# Optimizing a Trainium2 kernel written in Bass

```python
import numpy as np
import jax
import jax.numpy as jnp

def _softmax(x, axis=-1):
    return jax.nn.softmax(x, axis=axis)

def _gelu(x):
    return jax.nn.gelu(x, approximate=True)

def _silu(x):
    return jax.nn.silu(x)

def _sigmoid(x):
    return jax.nn.sigmoid(x)

def _layernorm(x, axis=-1, eps=1e-05):
    m = jnp.mean(x, axis=axis, keepdims=True)
    v = jnp.var(x, axis=axis, keepdims=True)
    return (x - m) / jnp.sqrt(v + eps)

def _scatter_add(tgt, idx, src, axis=0):
    return tgt.at[idx].add(src)

def _segment_sum(src, seg, n):
    return jax.ops.segment_sum(src, seg, n)
kernel_name = 'mk_xattn_ffn_d1_seqx_r8_94406b'

def setup_inputs(seed: int=0):
    np.random.seed(seed)
    _w = jnp.asarray

    def _rec_inputs():
        import jax
        import jax.numpy as jnp
        _rk = jax.random.key(seed)
        x = -7.109e-05 + 0.9999 * jax.random.normal(jax.random.fold_in(_rk, 1), (4, 256, 256), jnp.float32)
        _lenS = 256 - jax.random.randint(jax.random.fold_in(_rk, 7), (4,), 0, max(1, 256 // 4) + 1, jnp.int32)
        _lenS2 = 256 - jax.random.randint(jax.random.fold_in(_rk, 8), (4,), 0, max(1, 256 // 4) + 1, jnp.int32)
        _ctx_2048P = jax.random.normal(jax.random.fold_in(_rk, 11), (4, 16, 256), jnp.float32)
        _ctx_2048c = jax.random.dirichlet(jax.random.fold_in(_rk, 511), 0.3 * jnp.ones((16,), jnp.float32), (4, 256))
        _ctx_2048t = jnp.einsum('bsk,bkd->bsd', _ctx_2048c, _ctx_2048P)
        _ctx_2048t = _ctx_2048t * jax.lax.rsqrt(jnp.mean(jnp.square(_ctx_2048t)) + 1e-12) * 0.953939
        ctx_2048 = -3.05549e-07 + 0.0199987 * (_ctx_2048t + 0.3 * jax.random.normal(jax.random.fold_in(_rk, 611), (4, 256, 256), jnp.float32))
        return (x, ctx_2048)
    x, ctx_2048 = _rec_inputs()

    def _L0_xattn_setup():
        import jax, jax.numpy as jnp
        import numpy as np
        FP8_MAX = 448.0
        ACT_EPS = 0.0001
        W_EPS = 1e-06
        BLK = 128

        def quant_dequant_act_1x128(x):
            E, M, K = x.shape
            xb = x.reshape(E, M, K // BLK, BLK)
            amax = jnp.max(jnp.abs(xb), axis=-1, keepdims=True)
            safe = jnp.maximum(amax, ACT_EPS)
            q = (xb * (FP8_MAX / safe)).astype(jnp.float8_e4m3fn)
            return (q.astype(jnp.float32) * (safe / FP8_MAX)).reshape(E, M, K)

        def quant_dequant_weight_128x128(w):
            E, N, K = w.shape
            wb = w.reshape(E, N // BLK, BLK, K // BLK, BLK)
            amax = jnp.max(jnp.abs(wb), axis=(2, 4), keepdims=True)
            safe = jnp.maximum(amax, W_EPS)
            q = (wb * (FP8_MAX / safe)).astype(jnp.float8_e4m3fn)
            return (q.astype(jnp.float32) * (safe / FP8_MAX)).reshape(E, N, K)
        key = jax.random.key(seed)
        kx, kw = jax.random.split(key)
        E, M, K, N = (8, 512, 256, 256)
        x = jax.random.normal(kx, (E, M, K), dtype=jnp.float32)
        weight = jax.random.normal(kw, (E, N, K), dtype=jnp.float32) * 0.02
        return {'x': x, 'weight': weight}
    _L0_xattn_all = _L0_xattn_setup()
    _L0_xattn_in = {k: v for k, v in _L0_xattn_all.items() if k in ()}
    del _L0_xattn_all

    def _L0_ffn_setup():
        import jax, jax.numpy as jnp
        import numpy as np
        B, S, H = (1, 256, 256)
        I = 176
        E = 64
        TOP_K = 8
        N_GROUP = 8
        TOPK_GROUP = 4
        SCALE = 2.5
        N_SHARED = 2

        def _moe_forward(hidden_states, gate_w, e_bias, gate_proj, up_proj, down_proj, shared_gate_w, shared_up_w, shared_down_w):
            bsz, seq_len, h = hidden_states.shape
            xf = hidden_states.reshape(-1, h).astype(jnp.float32)
            T = bsz * seq_len
            logits = xf @ gate_w.T
            scores = jax.nn.sigmoid(logits)
            scores_for_choice = scores + e_bias[None, :]
            gs = scores_for_choice.reshape(T, N_GROUP, E // N_GROUP)
            group_scores = jax.lax.top_k(gs, 2)[0].sum(-1)
            group_idx = jax.lax.top_k(group_scores, TOPK_GROUP)[1]
            group_mask = jax.nn.one_hot(group_idx, N_GROUP, dtype=jnp.float32).sum(1)
            score_mask = jnp.repeat(group_mask, E // N_GROUP, axis=1)
            tmp_scores = jnp.where(score_mask > 0, scores_for_choice, 0.0)
            topk_idx = jax.lax.top_k(tmp_scores, TOP_K)[1]
            topk_w = jnp.take_along_axis(scores, topk_idx, axis=1)
            topk_w = topk_w / (topk_w.sum(-1, keepdims=True) + 1e-20)
            topk_w = topk_w * SCALE
            rows = jnp.arange(T)
            cw = jnp.zeros((T, E), jnp.float32).at[rows[:, None], topk_idx].add(topk_w)

            def step(y, we):
                Wg, Wu, Wd, w = we
                g = xf @ Wg.T
                u = xf @ Wu.T
                inter = jax.nn.silu(g) * u
                out = inter @ Wd.T
                return (y + out * w[:, None], None)
            y0 = jnp.zeros_like(xf)
            y, _ = jax.lax.scan(step, y0, (gate_proj, up_proj, down_proj, cw.T))
            y = y.reshape(bsz, seq_len, h)
            sg = hidden_states @ shared_gate_w.T
            su = hidden_states @ shared_up_w.T
            shared_out = jax.nn.silu(sg) * su @ shared_down_w.T
            return y + shared_out
        key = jax.random.key(seed)
        ks = jax.random.split(key, 9)
        x = jax.random.normal(ks[0], (B, S, H), dtype=jnp.float32)
        gate_w = jax.random.uniform(ks[1], (E, H), jnp.float32, -1.0, 1.0) / jnp.sqrt(float(H))
        e_bias = jnp.zeros((E,), jnp.float32)
        gate_proj = jax.random.normal(ks[2], (E, I, H), jnp.float32) * 0.02
        up_proj = jax.random.normal(ks[3], (E, I, H), jnp.float32) * 0.02
        down_proj = jax.random.normal(ks[4], (E, H, I), jnp.float32) * 0.02
        SI = I * N_SHARED
        shared_gate_w = jax.random.uniform(ks[5], (SI, H), jnp.float32, -1.0, 1.0) / jnp.sqrt(float(H))
        shared_up_w = jax.random.uniform(ks[6], (SI, H), jnp.float32, -1.0, 1.0) / jnp.sqrt(float(H))
        shared_down_w = jax.random.uniform(ks[7], (H, SI), jnp.float32, -1.0, 1.0) / jnp.sqrt(float(SI))
        return {'hidden_states': x, 'gate_w': gate_w, 'e_bias': e_bias, 'gate_proj': gate_proj, 'up_proj': up_proj, 'down_proj': down_proj, 'shared_gate_w': shared_gate_w, 'shared_up_w': shared_up_w, 'shared_down_w': shared_down_w}
    _L0_ffn_all = _L0_ffn_setup()
    _L0_ffn_in = {k: v for k, v in _L0_ffn_all.items() if k in ('gate_w', 'e_bias', 'gate_proj', 'up_proj', 'down_proj', 'shared_gate_w', 'shared_up_w', 'shared_down_w')}
    del _L0_ffn_all
    return {'x': x, 'ctx_2048': ctx_2048, 'L0_ffn_gate_w': _L0_ffn_in['gate_w'], 'L0_ffn_e_bias': _L0_ffn_in['e_bias'], 'L0_ffn_gate_proj': _L0_ffn_in['gate_proj'], 'L0_ffn_up_proj': _L0_ffn_in['up_proj'], 'L0_ffn_down_proj': _L0_ffn_in['down_proj'], 'L0_ffn_shared_gate_w': _L0_ffn_in['shared_gate_w'], 'L0_ffn_shared_up_w': _L0_ffn_in['shared_up_w'], 'L0_ffn_shared_down_w': _L0_ffn_in['shared_down_w']}

def reference(x, ctx_2048, L0_ffn_gate_w, L0_ffn_e_bias, L0_ffn_gate_proj, L0_ffn_up_proj, L0_ffn_down_proj, L0_ffn_shared_gate_w, L0_ffn_shared_up_w, L0_ffn_shared_down_w):
    import jax
    import jax.numpy as jnp

    def _L0_xattn_ref(x, weight):
        import jax, jax.numpy as jnp
        import numpy as np
        FP8_MAX = 448.0
        ACT_EPS = 0.0001
        W_EPS = 1e-06
        BLK = 128

        def quant_dequant_act_1x128(x):
            E, M, K = x.shape
            xb = x.reshape(E, M, K // BLK, BLK)
            amax = jnp.max(jnp.abs(xb), axis=-1, keepdims=True)
            safe = jnp.maximum(amax, ACT_EPS)
            q = (xb * (FP8_MAX / safe)).astype(jnp.float8_e4m3fn)
            return (q.astype(jnp.float32) * (safe / FP8_MAX)).reshape(E, M, K)

        def quant_dequant_weight_128x128(w):
            E, N, K = w.shape
            wb = w.reshape(E, N // BLK, BLK, K // BLK, BLK)
            amax = jnp.max(jnp.abs(wb), axis=(2, 4), keepdims=True)
            safe = jnp.maximum(amax, W_EPS)
            q = (wb * (FP8_MAX / safe)).astype(jnp.float8_e4m3fn)
            return (q.astype(jnp.float32) * (safe / FP8_MAX)).reshape(E, N, K)
        xq = quant_dequant_act_1x128(x)
        wq = quant_dequant_weight_128x128(weight)
        return jnp.einsum('emk,enk->emn', xq, wq)

    def _L0_ffn_ref(hidden_states, gate_w, e_bias, gate_proj, up_proj, down_proj, shared_gate_w, shared_up_w, shared_down_w):
        import jax, jax.numpy as jnp
        import numpy as np
        B, S, H = (1, 256, 256)
        I = 176
        E = 64
        TOP_K = 8
        N_GROUP = 8
        TOPK_GROUP = 4
        SCALE = 2.5
        N_SHARED = 2

        def _moe_forward(hidden_states, gate_w, e_bias, gate_proj, up_proj, down_proj, shared_gate_w, shared_up_w, shared_down_w):
            bsz, seq_len, h = hidden_states.shape
            xf = hidden_states.reshape(-1, h).astype(jnp.float32)
            T = bsz * seq_len
            logits = xf @ gate_w.T
            scores = jax.nn.sigmoid(logits)
            scores_for_choice = scores + e_bias[None, :]
            gs = scores_for_choice.reshape(T, N_GROUP, E // N_GROUP)
            group_scores = jax.lax.top_k(gs, 2)[0].sum(-1)
            group_idx = jax.lax.top_k(group_scores, TOPK_GROUP)[1]
            group_mask = jax.nn.one_hot(group_idx, N_GROUP, dtype=jnp.float32).sum(1)
            score_mask = jnp.repeat(group_mask, E // N_GROUP, axis=1)
            tmp_scores = jnp.where(score_mask > 0, scores_for_choice, 0.0)
            topk_idx = jax.lax.top_k(tmp_scores, TOP_K)[1]
            topk_w = jnp.take_along_axis(scores, topk_idx, axis=1)
            topk_w = topk_w / (topk_w.sum(-1, keepdims=True) + 1e-20)
            topk_w = topk_w * SCALE
            rows = jnp.arange(T)
            cw = jnp.zeros((T, E), jnp.float32).at[rows[:, None], topk_idx].add(topk_w)

            def step(y, we):
                Wg, Wu, Wd, w = we
                g = xf @ Wg.T
                u = xf @ Wu.T
                inter = jax.nn.silu(g) * u
                out = inter @ Wd.T
                return (y + out * w[:, None], None)
            y0 = jnp.zeros_like(xf)
            y, _ = jax.lax.scan(step, y0, (gate_proj, up_proj, down_proj, cw.T))
            y = y.reshape(bsz, seq_len, h)
            sg = hidden_states @ shared_gate_w.T
            su = hidden_states @ shared_up_w.T
            shared_out = jax.nn.silu(sg) * su @ shared_down_w.T
            return y + shared_out
        return _moe_forward(hidden_states, gate_w, e_bias, gate_proj, up_proj, down_proj, shared_gate_w, shared_up_w, shared_down_w)
    x = x + _L0_xattn_ref(_layernorm(x, axis=-1), ctx_2048)
    x = x + _L0_ffn_ref(_layernorm(x, axis=-1), L0_ffn_gate_w, L0_ffn_e_bias, L0_ffn_gate_proj, L0_ffn_up_proj, L0_ffn_down_proj, L0_ffn_shared_gate_w, L0_ffn_shared_up_w, L0_ffn_shared_down_w)
    return x

_drawn_inputs = setup_inputs


def setup_inputs(seed=0):
    import zlib

    import numpy as np

    out = dict(_drawn_inputs(seed))
    spreads = {'L0_ffn_e_bias': (0.0, 0.793)}
    factors = {'L0_ffn_gate_w': 5.398,
     'L0_ffn_gate_proj': 4.812,
     'L0_ffn_up_proj': 4.781,
     'L0_ffn_down_proj': 4.78}
    for name, (base, spread) in spreads.items():
        noise = np.random.default_rng([zlib.crc32(name.encode()), seed]).standard_normal(out[name].shape)
        drawn = base * np.exp(spread * noise) if base else spread * noise
        out[name] = jnp.asarray(drawn.astype(out[name].dtype))
    for name, factor in factors.items():
        out[name] = (out[name] * factor).astype(out[name].dtype)
    return out
```

```python
import concourse.bass as bass
from concourse import mybir
from contextlib import ExitStack


def xattn_moe_kernel(
    nc: bass.Bass,
    x: bass.AP,
    ctx_kn: bass.AP,
    gate_kn: bass.AP,
    e_bias: bass.AP,
    w_gu: bass.AP,
    w_down: bass.AP,
    ws_gu: bass.AP,
    ws_down: bass.AP,
    xfw: bass.AP,
    acc: list,
    out: bass.AP,
):
    fp32, bf16, fp16, i32 = mybir.dt.float32, mybir.dt.bfloat16, mybir.dt.float16, mybir.dt.int32
    ALU = mybir.AluOpType
    ACT = mybir.ActivationFunctionType
    X = mybir.AxisListType.X

    P = 128
    T, H = x.shape
    BATCH = ctx_kn.shape[0]
    E = gate_kn.shape[1]
    I = w_down.shape[1]
    GU = 2 * I
    C = T // P
    CPB = C // BATCH
    KB = H // P
    TOPK, NGROUP, TOPG = 8, 8, 4
    GSZ = E // NGROUP
    ROW = H + E
    LN_EPS, FP8_MAX, ACT_EPS, W_EPS, SCALE = 1e-5, 448.0, 1e-4, 1e-6, 2.5
    I0, I1 = 96, I - 96
    MAX_SLOTS = (T * TOPK + E * (P - 1)) // P
    R = 4
    QUADS = -(-MAX_SLOTS // R)
    AHEAD = R + 2
    COLS = R * QUADS + AHEAD
    HALF = 127.0 / 256.0
    ROUND = 1.5 * 2.0 ** 23

    ctx = ExitStack()
    with ctx:
        def sb(name, shape, dt=fp32):
            return ctx.enter_context(nc.sbuf_tensor(name, shape, dt))

        def sem(name):
            return ctx.enter_context(nc.semaphore(name))

        ident = sb("ident", [P, P])
        ident_bf = sb("ident_bf", [P, P], bf16)
        ones_bf = sb("ones_bf", [P, P], bf16)
        tri_bf = sb("tri_bf", [P, P], bf16)
        trie_bf = sb("trie_bf", [E, 2, E], bf16)
        ones_f = sb("ones_f", [P, P])
        tie = sb("tie", [P, NGROUP, NGROUP])
        iota_row = sb("iota_row", [P, COLS])
        part_pad = sb("part_pad", [P, 1])
        token1 = sb("token1", [P, C])
        zeros = sb("zeros", [P, ROW])
        x_sb = sb("x_sb", [P, C, H])
        c_sb = sb("c_sb", [P, BATCH * KB, H])
        gate_sb = sb("gate_sb", [P, KB, E])
        bias_sb = sb("bias_sb", [P, E])
        sgu_sb = sb("sgu_sb", [P, 2, KB * GU])
        sd0_sb = sb("sd0_sb", [I0, 2, H])
        sd1_sb = sb("sd1_sb", [I1, 2, H])
        stats = sb("stats", [P, C, 6])
        mv = sb("mv", [P, C, 2])
        var_e = sb("var_e", [P, C])
        std = sb("std", [P, C])
        rstd = sb("rstd", [P, C])
        nt = sb("nt", [P, C])
        early = sb("early", [P, 3 * C * H])
        ln = early[:, 0:C * H].rearrange("p (c h) -> p c h", c=C)
        qv = early[:, C * H:2 * C * H]
        qm = early[:, 2 * C * H:3 * C * H]
        xq = sb("xq", [P, C, H], bf16)
        cq = sb("cq", [P, BATCH * KB, H], bf16)
        amax = sb("amax", [P, C * KB])
        qs = sb("qs", [P, C * KB])
        dq = sb("dq", [P, C * KB])
        camax = sb("camax", [P, C * KB])
        cmx = sb("cmx", [16, 1])
        cdiag = sb("cdiag", [16, 16])
        cqs = sb("cqs", [P, C * KB])
        cdq = sb("cdq", [P, C * KB])
        dqq = sb("dqq", [P, C, KB, KB])
        xqT = sb("xqT", [P, C, KB, P], bf16)
        x1 = sb("x1", [P, C, H])
        xf = sb("xf", [P, C, H])
        xfT = sb("xfT", [P, C, KB, P])
        scores = sb("scores", [P, C, E])
        choice = sb("choice", [P, C, E])
        gtop = sb("gtop", [P, C * NGROUP, 8])
        gsc = sb("gsc", [P, C, NGROUP])
        gcmp = sb("gcmp", [P, C, NGROUP, NGROUP])
        geq = sb("geq", [P, C, NGROUP, NGROUP])
        grank = sb("grank", [P, C * NGROUP])
        gmask = sb("gmask", [P, C * NGROUP])
        masked = sb("masked", [P, C, E])
        top8 = sb("top8", [P, C, 8])
        replaced = sb("replaced", [P, C, E])
        mask = sb("mask", [P, C, E])
        mask_bf = sb("mask_bf", [P, C, E], bf16)
        cw = sb("cw", [P, C, E])
        wsum = sb("wsum", [P, C])
        winv = sb("winv", [P, C])
        cnt = sb("cnt", [E, 1])
        ntl = sb("ntl", [E, 1])
        ntl_bf = sb("ntl_bf", [E, P], bf16)
        base = sb("base", [P, E])
        cum_col = sb("cum_col", [E, 1])
        pos = sb("pos", [P, C, E])
        pos8 = sb("pos8", [P, C, 8])
        posj = sb("posj", [P, C, 8])
        posp = sb("posp", [P, C, 8])
        posj_h = sb("posj_h", [P, C, 8], fp16)
        posp_h = sb("posp_h", [P, C, 8], fp16)
        iota_k = sb("iota_k", [P, COLS, TOPK], fp16)
        oh_p = sb("oh_p", [P, C, P, TOPK], fp16)
        oh_s = early[:, 0:C * 8 * COLS // 2].bitcast(fp16).rearrange("p (c j k) -> p c j k", c=C, k=TOPK)
        oh_j = sb("oh_j", [P, C, COLS, TOPK], fp16)
        slot_ge = sb("slot_ge", [E, COLS])
        padv = sb("padv", [P, COLS])
        idx_tab = sb("idx_tab", [P, COLS], i32)
        slot_tab = sb("slot_tab", [1, COLS + 1], i32)
        quads_f = sb("quads_f", [1, 2])
        s_silu = sb("s_silu", [P, 2, I])
        s_up = sb("s_up", [P, 2, I])
        s_int = sb("s_int", [P, 2, I])
        s_iT = sb("s_iT", [I0, 2, 2, P])
        s_out = sb("s_out", [P, 2, H])
        fin = sb("fin", [P, C, H])
        gu_ring = sb("gu_ring", [P, R, KB * GU])
        d0_ring = sb("d0_ring", [I0, R, H])
        d1_ring = sb("d1_ring", [I1, R, H])
        rows = sb("rows", [P, R, ROW])
        wcol = sb("wcol", [P, R])
        gidx = sb("gidx", [P, R], i32)
        sidx = sb("sidx", [P, R], i32)
        rT = sb("rT", [P, 2, KB, P])
        silu = sb("silu", [P, 2, I])
        inter = sb("inter", [P, 2, I])
        iT = sb("iT", [I0, 2, 2, P])
        y = sb("y", [P, R, H])
        y0, y1 = x_sb, c_sb

        bank = [ctx.enter_context(nc.psum_tensor(f"bank{b}", [P, 512], fp32)) for b in range(8)]
        XT, GB, IT, OB = bank[0:2], bank[2:4], bank[4:6], bank[6:8]

        ld_x, ld_c, ld_gate, ld_bias, ld_sh = (sem(n) for n in ("ld_x", "ld_c", "ld_gate", "ld_bias", "ld_sh"))
        made = sem("made")
        dve = sem("dve")
        ln_var, ln_std = sem("ln_var"), sem("ln_std")
        camax_ok, camaxT_ok, cmx_ok, cbc_ok = (sem(n) for n in ("camax_ok", "camaxT_ok", "cmx_ok", "cbc_ok"))
        xq_ok, xqT_ps, xqT_ok, att_ps, att_used = (sem(n) for n in ("xq_ok", "xqT_ps", "xqT_ok", "att_ps", "att_used"))
        xf_ok, xfT_ps, xfT_ok, logit_ps, score_ok = (sem(n) for n in ("xf_ok", "xfT_ps", "xfT_ok", "logit_ps", "score_ok"))
        mask_ok, cnt_ps, ntl_ok, cum_ps = (sem(n) for n in ("mask_ok", "cnt_ps", "ntl_ok", "cum_ps"))
        ohs_ok, ohj_ok, ohp_ok = (sem(n) for n in ("ohs_ok", "ohj_ok", "ohp_ok"))
        tab_ps, ge_ok, slot_ps, tabs_ok = (sem(n) for n in ("tab_ps", "ge_ok", "slot_ps", "tabs_ok"))
        rows_st, cw_ok, zero_ok = sem("rows_st"), sem("cw_ok"), sem("zero_ok")
        sh_gu, sh_act, sh_int, sh_iT, sh_iTc, sh_out, sh_outc, sh_fin = (
            sem(n) for n in ("sh_gu", "sh_act", "sh_int", "sh_iT", "sh_iTc", "sh_out", "sh_outc", "sh_fin"))
        row_in = [sem(f"row_in{r}") for r in range(R)]
        gu_in = [sem(f"gu_in{r}") for r in range(R)]
        d_in = [sem(f"d_in{r}") for r in range(R)]
        acc_in = [sem(f"acc_in{a}") for a in range(2)]
        pool_go = sem("pool_go")
        wcol_ok = sem("wcol_ok")
        gidx_ok, sidx_ok = sem("gidx_ok"), sem("sidx_ok")
        rT_ps, rT_ok, gu_ps, silu_ok, inter_ok, iT_ps, iT_ok, out_ps, y_ok = (
            sem(n) for n in ("rT_ps", "rT_ok", "gu_ps", "silu_ok", "inter_ok", "iT_ps", "iT_ok", "out_ps", "y_ok"))
        acc_ld = [sem(f"acc_ld{c}") for c in range(C)]
        y_sum, done = sem("y_sum"), sem("done")

        block = ctx.enter_context(nc.Block())

        def chunks(dram, cols=None):
            return dram[0:T, 0:(cols or dram.shape[1])].rearrange("(c p) h -> p c h", p=P)

        MADE = 17

        def expert_of(eng, slot):
            return eng.value_load(slot_tab[0:1, bass.ds(slot, 1)], min_val=0, max_val=E - 1)

        def load_gu(eng, e, r):
            eng.dma_start(gu_ring[:, r, :], w_gu[bass.ds(e, 1), :, :].rearrange("a p n -> (a p) n")).then_inc(gu_in[r], 16)

        def load_down(eng, e, r):
            eng.dma_start(d0_ring[:, r, :], w_down[bass.ds(e, 1), 0:I0, :].rearrange("a i h -> (a i) h")).then_inc(d_in[r], 16)
            eng.dma_start(d1_ring[:, r, :], w_down[bass.ds(e, 1), I0:I, :].rearrange("a i h -> (a i) h")).then_inc(d_in[r], 16)

        def quads_of(eng):
            return eng.value_load(slot_tab[0:1, COLS:COLS + 1], min_val=1, max_val=QUADS)

        ONE_HOTS_AT = {8: [0, 1, 2], 9: [3, 4, 5], 10: [6, 7]}
        FIRST_ROWS_AT = 12

        def gather(pool, r):
            pool.wait_ge(rows_st, 48)
            pool.sem_inc(pool_go, 1)
            pool.indirect_dma_start(
                out=rows[:, r, :], out_offset=None, in_=xfw,
                in_offset=bass.IndirectOffsetOnAxis(ap=gidx[:, r:r + 1], axis=0),
                bounds_check=T + P - 1, oob_is_err=True).then_inc(row_in[r], 16)

        def add_chunk(pool, c):
            pool.wait_ge(sh_outc, c + 1)
            pool.tensor_tensor(fin[:, c, :], s_out[:, c % 2, :], x1[:, c, :], ALU.add).then_inc(sh_fin, 1)

        def copy_iT(eng, to, b):
            eng.activation(to[0:I0, b, 0, :], IT[b][0:I0, 0:P], ACT.Copy)
            return eng.activation(to[0:I1, b, 1, :], IT[b][0:I1, P:2 * P], ACT.Copy)

        def shared_out(act, c):
            act.wait_ge(sh_out, c + 1)
            if c >= 2:
                act.wait_ge(sh_fin, c - 1)
            act.activation(s_out[:, c % 2, :], OB[c % 2][:, 0:H], ACT.Copy).then_inc(sh_outc, 1)

        def copy_rows(v, e, r, b):
            v.tensor_copy(wcol[:, r:r + 1], rows[:, r, bass.ds(e + H, 1)]).then_inc(wcol_ok, 1)
            v.tensor_copy(rT[:, b, :, :], XT[b][:, 0:H].rearrange("p (k t) -> p k t", k=KB)).then_inc(rT_ok, 1)

        def combine(v, r, count):
            v.wait_ge(silu_ok, count)
            v.wait_ge(wcol_ok, count)
            v.scalar_tensor_tensor(inter[:, r % 2, :], silu[:, r % 2, :], wcol[:, r:r + 1],
                                   GB[r % 2][:, I:GU], ALU.mult, ALU.mult).then_inc(inter_ok, 1)

        def turn(pe, src, b, to):
            pe.transpose(to[0:I0, 0:P], src[:, b, 0:I0], ident[:, :])
            return pe.transpose(to[0:I1, P:2 * P], src[:, b, I0:I], ident[:, :])

        @block.sync
        def _(sp):
            sp.dma_start(x_sb[:, :, :], chunks(x)).then_inc(ld_x, 16)
            sp.dma_start(gate_sb[:, :, :], gate_kn.rearrange("(k p) e -> p k e", p=P)).then_inc(ld_gate, 16)
            sp.dma_start(bias_sb[:, :], e_bias.partition_broadcast(P)).then_inc(ld_bias, 16)
            sp.dma_start(sgu_sb[:, :, :], ws_gu.rearrange("a p n -> p a n")).then_inc(ld_sh, 16)
            sp.dma_start(sd0_sb[:, :, :], ws_down[:, 0:I0, :].rearrange("a i h -> i a h")).then_inc(ld_sh, 16)
            sp.dma_start(sd1_sb[:, :, :], ws_down[:, I0:I, :].rearrange("a i h -> i a h")).then_inc(ld_sh, 16)
            sp.wait_ge(made, MADE)
            sp.dma_start(xfw[T:T + P, :], zeros[:, :]).then_inc(rows_st, 16)
            sp.wait_ge(xf_ok, C)
            sp.dma_start(chunks(xfw, H), xf[:, :, :]).then_inc(rows_st, 16)
            sp.wait_ge(cw_ok, 1)
            sp.dma_start(xfw[0:T, H:ROW].rearrange("(c p) h -> p c h", p=P), cw[:, :, :]).then_inc(rows_st, 16)
            sp.wait_ge(tabs_ok, 1)
            for r in range(R):
                e = expert_of(sp, r)
                load_gu(sp, e, r)
                load_down(sp, e, r)
            quads = quads_of(sp)
            with sp.Fori(0, QUADS) as i:
                with sp.If(i < quads):
                    for r in range(R):
                        e = expert_of(sp, i * R + (r + R))
                        sp.wait_ge(gu_ps, i * R + (r + 1))
                        load_gu(sp, e, r)
                        sp.wait_ge(out_ps, i * R + (r + 1))
                        load_down(sp, e, r)
            for r in range(R):
                sp.wait_ge(gu_in[r], quads * 16 + 16)
                sp.wait_ge(d_in[r], quads * 32 + 32)
            for a in range(2):
                sp.wait_ge(acc_in[a], quads * (16 * R // 2) + 32)
            for c in range(C):
                sp.dma_start(y0[:, c, :], acc[0][c * P:(c + 1) * P, :]).then_inc(acc_ld[c], 16)
                sp.dma_start(y1[:, c, :], acc[1][c * P:(c + 1) * P, :]).then_inc(acc_ld[c], 16)
            for c in range(C):
                sp.wait_ge(y_sum, c + 1)
                sp.dma_start(out[c * P:(c + 1) * P, :], y0[:, c, :]).then_inc(done, 16)
            sp.wait_ge(done, 16 * C)

        @block.gpsimd
        def _(pool):
            steps = [0]

            def step(ins):
                steps[0] += 1
                ins.then_inc(made, 1)

            def cut(t, pattern, mult, op, fill):
                pool.affine_select(out=t, in_=t, compare_op=op, fill=fill, base=0, pattern=pattern,
                                   channel_multiplier=mult).then_inc(made, 1)
                steps[0] += 1

            step(pool.memset(ident[:, :], 0.0))
            step(pool.memset(ident_bf[:, :], 0.0))
            step(pool.memset(tri_bf[:, :], 1.0))
            step(pool.memset(trie_bf[:, :, :], 1.0))
            step(pool.memset(tie[:, :, :], 1.0))
            step(pool.memset(ones_bf[:, :], 1.0))
            step(pool.memset(ones_f[:, :], 1.0))
            step(pool.memset(zeros[:, :], 0.0))
            pool.wait_ge(made, steps[0])
            cut(ident[:, :], [[-1, P]], 1, ALU.not_equal, 1.0)
            cut(ident_bf[:, :], [[-1, P]], 1, ALU.not_equal, 1.0)
            cut(tri_bf[:, :], [[1, P]], -1, ALU.is_gt, 0.0)
            cut(trie_bf[:, :, :], [[-1, 2], [1, E]], -1, ALU.is_ge, 0.0)
            cut(tie[:, :, :], [[1, NGROUP], [-1, NGROUP]], 0, ALU.is_gt, 0.0)
            step(pool.iota(iota_row[:, :], pattern=[[1, COLS]], base=0, channel_multiplier=0,
                           allow_small_or_imprecise_dtypes=True))
            step(pool.iota(iota_k[:, :, :], pattern=[[1, COLS], [0, TOPK]], base=0, channel_multiplier=0,
                           allow_small_or_imprecise_dtypes=True))
            step(pool.iota(part_pad[:, :], pattern=[[0, 1]], base=T + 1, channel_multiplier=1,
                           allow_small_or_imprecise_dtypes=True))
            step(pool.iota(token1[:, :], pattern=[[P, C]], base=1, channel_multiplier=1,
                           allow_small_or_imprecise_dtypes=True))
            assert steps[0] == MADE
            for a in range(2):
                pool.dma_start(acc[a][T:T + P, :], zeros[:, 0:H]).then_inc(acc_in[a], 16)
            pool.dma_start(chunks(acc[1]), zeros[:, 0:H].unsqueeze(1).to_broadcast([P, C, H])).then_inc(acc_in[1], 16)
            for u in range(2 * C):
                pool.wait_ge(sh_act, 2 * (u + 1))
                pool.tensor_tensor(s_int[:, u % 2, :], s_silu[:, u % 2, :], s_up[:, u % 2, :], ALU.mult).then_inc(sh_int, 1)
                if u % 2 == 0 and u >= 4:
                    add_chunk(pool, u // 2 - 2)
                if u == FIRST_ROWS_AT:
                    for r in range(R):
                        pool.wait_ge(gidx_ok, r + 1)
                        gather(pool, r)
            add_chunk(pool, C - 2)
            add_chunk(pool, C - 1)
            pool.wait_ge(sh_fin, C)
            pool.dma_start(chunks(acc[0]), fin[:, :, :]).then_inc(acc_in[0], 16)
            for f in range(2):
                pool.wait_ge(gidx_ok, R + f + 1)
                gather(pool, f)
            quads = quads_of(pool)
            with pool.Fori(0, QUADS) as i:
                with pool.If(i < quads):
                    for r in range(R):
                        pool.wait_ge(rT_ok, i * R + (r + 3))
                        pool.wait_ge(gidx_ok, i * R + (r + AHEAD + 1))
                        gather(pool, (r + 2) % R)
                        pool.wait_ge(sidx_ok, i * R + (r + 1))
                        pool.wait_ge(y_ok, i * R + (r + 1))
                        pool.wait_ge(acc_in[r % 2], i * (16 * R // 2) + (32 + 16 * (r // 2)))
                        pool.sem_inc(pool_go, 1)
                        pool.indirect_dma_start(
                            out=acc[r % 2], out_offset=bass.IndirectOffsetOnAxis(ap=sidx[:, r:r + 1], axis=0),
                            in_=y[:, r, :], in_offset=None, bounds_check=T + P - 1, oob_is_err=True,
                            compute_op=ALU.add).then_inc(acc_in[r % 2], 16)
            for r in range(R):
                pool.wait_ge(row_in[r], quads * 16 + (32 if r < 2 else 16))

        @block.scalar
        def _(act):
            act.dma_start(c_sb[:, :, :], ctx_kn.rearrange("b (k p) n -> p (b k) n", p=P)).then_inc(ld_c, 16)
            act.wait_ge(ln_var, 1)
            act.activation(std[:, :], var_e[:, :], ACT.Sqrt).then_inc(ln_std, 1)
            for b in range(2):
                act.wait_ge(xqT_ps, b + 1)
                act.activation(xqT[:, 4 * b:4 * b + 4, :, :], bank[2 + b][:, :].bitcast(bf16).rearrange(
                    "p (c k t) -> p c k t", c=4, k=KB), ACT.Copy).then_inc(xqT_ok, 1)
            act.wait_ge(ln_var, 2)
            act.activation(std[:, :], var_e[:, :], ACT.Sqrt).then_inc(ln_std, 1)
            for b in range(C // 2):
                act.wait_ge(xfT_ps, b + 1)
                act.activation(xfT[:, 2 * b:2 * b + 2, :, :], bank[b][:, :].rearrange(
                    "p (c k t) -> p c k t", c=2, k=KB), ACT.Copy).then_inc(xfT_ok, 1)
            act.wait_ge(logit_ps, 1)
            act.activation(scores[:, :, :], bank[4][:, :].rearrange("p (c e) -> p c e", c=C), ACT.Sigmoid).then_inc(score_ok, 1)
            for u in range(2 * C):
                act.wait_ge(sh_gu, u + 1)
                if u >= 2:
                    act.wait_ge(sh_int, u - 1)
                act.activation(s_silu[:, u % 2, :], GB[u % 2][:, 0:I], ACT.Silu).then_inc(sh_act, 1)
                act.activation(s_up[:, u % 2, :], GB[u % 2][:, I:GU], ACT.Copy).then_inc(sh_act, 1)
                act.wait_ge(sh_iT, u + 1)
                copy_iT(act, s_iT, u % 2).then_inc(sh_iTc, 1)
                if u % 2 == 0 and u >= 4:
                    shared_out(act, u // 2 - 2)
                if u in ONE_HOTS_AT:
                    for c in ONE_HOTS_AT[u]:
                        act.wait_ge(ohs_ok, c + 1)
                        act.activation(oh_j[:, c, :, :], oh_s[:, c, :, :], ACT.Copy,
                                       scale=token1[:, c:c + 1]).then_inc(ohj_ok, 1)
            shared_out(act, C - 2)
            shared_out(act, C - 1)
            act.wait_ge(gu_ps, 1)
            act.activation(silu[:, 0, :], GB[0][:, 0:I], ACT.Silu).then_inc(silu_ok, 1)
            act.wait_ge(tabs_ok, 1)
            quads = quads_of(act)
            with act.Fori(0, QUADS) as i:
                with act.If(i < quads):
                    for r in range(R):
                        act.wait_ge(iT_ps, i * R + (r + 1))
                        copy_iT(act, iT, r % 2).then_inc(iT_ok, 1)
                        act.wait_ge(gu_ps, i * R + (r + 2))
                        act.activation(silu[:, (r + 1) % 2, :], GB[(r + 1) % 2][:, 0:I], ACT.Silu).then_inc(silu_ok, 1)

        @block.vector
        def _(v):
            made_by = [0]

            def step(ins):
                made_by[0] += 1
                ins.then_inc(dve, 1)

            def settle():
                v.wait_ge(dve, made_by[0])

            def norm_stats(src, n):
                for c in range(C):
                    step(v.bn_stats(stats[:, c, :], src[:, c, :]))
                settle()
                for c in range(C):
                    step(v.bn_aggr(mv[:, c, :], stats[:, c, :]))
                settle()
                v.tensor_scalar(var_e[:, :], mv[:, :, 1], LN_EPS, None, ALU.add).then_inc(ln_var, 1)
                v.wait_ge(ln_var, n)
                v.wait_ge(ln_std, n)
                step(v.reciprocal(rstd[:, :], std[:, :]))
                settle()
                step(v.tensor_tensor(nt[:, :], rstd[:, :], rstd[:, :], ALU.mult))
                settle()
                step(v.tensor_tensor(nt[:, :], nt[:, :], var_e[:, :], ALU.mult))
                settle()
                step(v.tensor_scalar(nt[:, :], nt[:, :], -0.5, 1.5, ALU.mult, ALU.add))
                settle()
                step(v.tensor_tensor(rstd[:, :], rstd[:, :], nt[:, :], ALU.mult))
                settle()

            def normalise(dst, src, c):
                return v.tensor_scalar(dst[:, c, :], src[:, c, :], mv[:, c, 0:1], rstd[:, c:c + 1],
                                       ALU.subtract, ALU.mult)

            def quantise(dst, src, scale):
                seg = "p (s n) -> p s n"
                step(v.tensor_tensor(qv[:, :].rearrange(seg, n=P), src, scale.unsqueeze(2).to_broadcast([P, C * KB, P]), ALU.mult))
                settle()
                step(v.tensor_scalar(qm[:, :].bitcast(i32), qv[:, :].bitcast(i32), 0x7F800000, None, ALU.bitwise_and))
                settle()
                step(v.tensor_scalar(qm[:, :], qm[:, :], 2.0 ** -6, 1.5 * 2.0 ** 20, ALU.max, ALU.mult))
                settle()
                step(v.tensor_tensor(qv[:, :], qv[:, :], qm[:, :], ALU.add))
                settle()
                return v.tensor_tensor(dst, qv[:, :].rearrange(seg, n=P), qm[:, :].rearrange(seg, n=P), ALU.subtract)

            def scales(src, floor, mul, div):
                step(v.tensor_scalar(div[:, :], src, floor, None, ALU.max))
                settle()
                step(v.reciprocal(mul[:, :], div[:, :]))
                settle()
                step(v.tensor_scalar(mul[:, :], mul[:, :], FP8_MAX, None, ALU.mult))
                step(v.tensor_scalar(div[:, :], div[:, :], 1.0 / FP8_MAX, None, ALU.mult))
                settle()

            v.wait_ge(ld_c, 16)
            v.tensor_reduce(camax[:, :], c_sb[:, :, :].rearrange("p a (n m) -> p (a n) m", m=P), X, ALU.max,
                            apply_absolute_value=True).then_inc(camax_ok, 1)
            v.wait_ge(camaxT_ok, 1)
            step(v.tensor_reduce(cmx[:, :], bank[0][0:16, 0:P], X, ALU.max))
            settle()
            v.tensor_scalar(cdiag[:, :], ident[0:16, 0:16], cmx[:, 0:1], None, ALU.mult).then_inc(cmx_ok, 1)
            v.wait_ge(cbc_ok, 1)
            scales(bank[1][:, 0:C * KB], W_EPS, cqs, cdq)
            step(quantise(cq[:, :, :].rearrange("p a (n m) -> p (a n) m", m=P),
                          c_sb[:, :, :].rearrange("p a (n m) -> p (a n) m", m=P), cqs[:, :]))
            v.wait_ge(ld_x, 16)
            norm_stats(x_sb, 1)
            for c in range(C):
                step(normalise(ln, x_sb, c))
            settle()
            step(v.tensor_reduce(amax[:, :], ln[:, :, :].rearrange("p c (k m) -> p (c k) m", m=P), X, ALU.max,
                                 apply_absolute_value=True))
            settle()
            scales(amax[:, :], ACT_EPS, qs, dq)
            quantise(xq[:, :, :].rearrange("p c (k m) -> p (c k) m", m=P),
                     ln[:, :, :].rearrange("p c (k m) -> p (c k) m", m=P), qs[:, :]).then_inc(xq_ok, 1)
            for h in range(CPB):
                step(v.tensor_tensor(
                    dqq[:, h::CPB, :, :], dq[:, :].rearrange("p (c k) -> p c k", k=KB)[:, h::CPB, :].unsqueeze(3)
                    .to_broadcast([P, BATCH, KB, KB]), cdq[:, :].rearrange("p (b k n) -> p b k n", b=BATCH, k=KB), ALU.mult))
            settle()
            for c in range(C):
                v.wait_ge(att_ps, c + 1)
                ps = bank[4 + c % 4][:, :].rearrange("p (k n) -> p k n", k=KB)
                for k in range(KB):
                    for n in range(KB):
                        cols = slice(n * P, (n + 1) * P)
                        ins = v.scalar_tensor_tensor(x1[:, c, cols], ps[:, k, cols], dqq[:, c, k, n:n + 1],
                                                     (x_sb if k == 0 else x1)[:, c, cols], ALU.mult, ALU.add)
                        if (k, n) == (KB - 1, KB - 1):
                            ins.then_inc(att_used, 1)
                        else:
                            step(ins)
                    if k == 0:
                        settle()
            v.wait_ge(att_used, C)
            settle()
            norm_stats(x1, 2)
            for c in range(C):
                normalise(xf, x1, c).then_inc(xf_ok, 1)

            v.wait_ge(score_ok, 1)
            v.wait_ge(ld_bias, 16)
            step(v.tensor_tensor(choice[:, :, :], scores[:, :, :], bias_sb[:, :].unsqueeze(1).to_broadcast([P, C, E]), ALU.add))
            settle()
            for c in range(C):
                for g in range(NGROUP):
                    step(v.max(gtop[:, c * NGROUP + g, :], choice[:, c, g * GSZ:(g + 1) * GSZ]))
            settle()
            step(v.tensor_tensor(gsc[:, :, :].rearrange("p c g -> p (c g)"), gtop[:, :, 0], gtop[:, :, 1], ALU.add))
            settle()
            shape = [P, C, NGROUP, NGROUP]
            other, own = gsc[:, :, :].unsqueeze(2).to_broadcast(shape), gsc[:, :, :].unsqueeze(3).to_broadcast(shape)
            step(v.tensor_tensor(gcmp[:, :, :, :], other, own, ALU.is_gt))
            step(v.tensor_tensor(geq[:, :, :, :], other, own, ALU.is_equal))
            settle()
            step(v.tensor_tensor(geq[:, :, :, :], geq[:, :, :, :], tie[:, :, :].unsqueeze(1).to_broadcast(shape), ALU.mult))
            settle()
            step(v.tensor_tensor(gcmp[:, :, :, :], gcmp[:, :, :, :], geq[:, :, :, :], ALU.add))
            settle()
            step(v.tensor_reduce(grank[:, :], gcmp[:, :, :, :].rearrange("p c g o -> p (c g) o"), X, ALU.add))
            settle()
            step(v.tensor_scalar(gmask[:, :], grank[:, :], float(TOPG), None, ALU.is_lt))
            settle()
            step(v.tensor_tensor(masked[:, :, :].rearrange("p c (g s) -> p (c g) s", s=GSZ),
                                 choice[:, :, :].rearrange("p c (g s) -> p (c g) s", s=GSZ),
                                 gmask[:, :].unsqueeze(2).to_broadcast([P, C * NGROUP, GSZ]), ALU.mult))
            settle()
            for c in range(C):
                step(v.max(top8[:, c, :], masked[:, c, :]))
            settle()
            for c in range(C):
                step(v.match_replace(replaced[:, c, :], top8[:, c, :], masked[:, c, :], -3.0e38))
            settle()
            v.tensor_tensor(mask_bf[:, :, :], replaced[:, :, :], masked[:, :, :], ALU.not_equal).then_inc(mask_ok, 1)
            step(v.tensor_tensor(mask[:, :, :], replaced[:, :, :], masked[:, :, :], ALU.not_equal))
            settle()
            v.wait_ge(cnt_ps, 1)
            step(v.tensor_scalar(cnt[:, :], bank[1][0:E, 0:1], 1.0 / P, (P - 1.0) / P - HALF, ALU.mult, ALU.add))
            settle()
            step(v.tensor_scalar(ntl[:, :], cnt[:, :], ROUND, ROUND, ALU.add, ALU.subtract))
            settle()
            v.tensor_copy(ntl_bf[:, :], ntl[:, 0:1].to_broadcast([E, P])).then_inc(ntl_ok, 1)
            v.wait_ge(cum_ps, 1)
            step(v.tensor_scalar(base[:, :], bank[1][:, E:2 * E], float(P), 1.0, ALU.mult, ALU.add))
            step(v.tensor_copy(cum_col[:, :], bank[1][0:E, 2 * E:2 * E + 1]))
            step(v.tensor_scalar(quads_f[:, 0:1], bank[1][0:1, E - 1:E], 1.0 / R, (R - 1.0) / R - 0.375, ALU.mult, ALU.add))
            settle()
            step(v.tensor_tensor(pos[:, :, :], bank[0][:, :].rearrange("p (c e) -> p c e", c=C),
                                 base[:, :].unsqueeze(1).to_broadcast([P, C, E]), ALU.add))
            v.tensor_scalar(slot_ge[:, :], iota_row[0:E, :], cum_col[:, 0:1], None, ALU.is_ge).then_inc(ge_ok, 1)
            settle()
            step(v.tensor_tensor(pos[:, :, :], pos[:, :, :], mask[:, :, :], ALU.mult))
            settle()
            for c in range(C):
                step(v.max(pos8[:, c, :], pos[:, c, :]))
            settle()
            step(v.tensor_scalar(posj[:, :, :], pos8[:, :, :], 1.0 / P, -1.0 / P - HALF, ALU.mult, ALU.add))
            settle()
            step(v.tensor_scalar(posj[:, :, :], posj[:, :, :], ROUND, ROUND, ALU.add, ALU.subtract))
            settle()
            step(v.tensor_copy(posj_h[:, :, :], posj[:, :, :]))
            step(v.tensor_scalar(posp[:, :, :], posj[:, :, :], -float(P), -1.0, ALU.mult, ALU.add))
            settle()
            step(v.tensor_tensor(posp_h[:, :, :], posp[:, :, :], pos8[:, :, :], ALU.add))
            settle()
            for c in range(C):
                v.tensor_tensor(oh_s[:, c, :, :], posj_h[:, c, :].unsqueeze(1).to_broadcast([P, COLS, TOPK]),
                                iota_k[:, :, :], ALU.is_equal).then_inc(ohs_ok, 1)
                v.tensor_tensor(oh_p[:, c, :, :], posp_h[:, c, :].unsqueeze(1).to_broadcast([P, P, TOPK]),
                                iota_k[:, 0:P, :], ALU.is_equal).then_inc(ohp_ok, 1)
            step(v.tensor_tensor(cw[:, :, :], scores[:, :, :], mask[:, :, :], ALU.mult))
            settle()
            step(v.tensor_reduce(wsum[:, :], cw[:, :, :], X, ALU.add))
            settle()
            step(v.tensor_scalar(wsum[:, :], wsum[:, :], 1e-20, None, ALU.add))
            settle()
            step(v.reciprocal(winv[:, :], wsum[:, :]))
            settle()
            step(v.tensor_scalar(winv[:, :], winv[:, :], SCALE, None, ALU.mult))
            settle()
            v.tensor_tensor(cw[:, :, :], cw[:, :, :], winv[:, :].unsqueeze(2).to_broadcast([P, C, E]), ALU.mult).then_inc(cw_ok, 1)
            v.wait_ge(slot_ps, 1)
            step(v.tensor_scalar(slot_tab[:, 0:COLS], bank[1][0:1, 256:256 + COLS], E - 1.0, None, ALU.min))
            step(v.tensor_scalar(slot_tab[:, COLS:COLS + 1], quads_f[:, 0:1], ROUND, ROUND, ALU.add, ALU.subtract))
            v.wait_ge(tab_ps, 1)
            step(v.tensor_scalar(padv[:, :], bank[0][:, 0:COLS], 0.0, part_pad[:, 0:1], ALU.is_equal, ALU.mult))
            settle()
            v.scalar_tensor_tensor(idx_tab[:, :], bank[0][:, 0:COLS], -1.0, padv[:, :], ALU.add, ALU.add).then_inc(tabs_ok, 1)

            v.wait_ge(tabs_ok, 1)
            for r in range(R):
                v.tensor_copy(gidx[:, r:r + 1], idx_tab[:, r:r + 1]).then_inc(gidx_ok, 1)
            quads = quads_of(v)
            for f in range(2):
                v.wait_ge(rT_ps, f + 1)
                copy_rows(v, expert_of(v, f), f, f)
                v.tensor_copy(gidx[:, f:f + 1], idx_tab[:, R + f:R + f + 1]).then_inc(gidx_ok, 1)
            combine(v, 0, 1)
            with v.Fori(0, QUADS) as i:
                with v.If(i < quads):
                    for r in range(R):
                        e = expert_of(v, i * R + (r + 2))
                        v.wait_ge(acc_in[r % 2], i * (16 * R // 2) + 16 * (r // 2 + 1))
                        v.tensor_copy(sidx[:, r:r + 1], idx_tab[:, bass.ds(i * R + r, 1)]).then_inc(sidx_ok, 1)
                        v.wait_ge(rT_ps, i * R + (r + 3))
                        g = (r + 2) % R
                        v.tensor_copy(gidx[:, g:g + 1], idx_tab[:, bass.ds(i * R + (r + AHEAD), 1)]).then_inc(gidx_ok, 1)
                        copy_rows(v, e, g, r % 2)
                        combine(v, (r + 1) % R, i * R + (r + 2))
                        v.wait_ge(out_ps, i * R + (r + 1))
                        v.tensor_copy(y[:, r, :], OB[r % 2][:, 0:H]).then_inc(y_ok, 1)
            for c in range(C):
                v.wait_ge(acc_ld[c], 32)
                v.tensor_tensor(y0[:, c, :], y0[:, c, :], y1[:, c, :], ALU.add).then_inc(y_sum, 1)

        @block.tensor
        def _(pe):
            pe.wait_ge(made, MADE)
            pe.wait_ge(camax_ok, 1)
            pe.transpose(bank[0][0:16, 0:P], camax[:, :], ident[:, :]).then_inc(camaxT_ok, 1)
            pe.wait_ge(cmx_ok, 1)
            pe.matmul(bank[1][:, 0:16], ones_f[0:16, :], cdiag[:, :], start=True, stop=True).then_inc(cbc_ok, 1)
            pe.wait_ge(xq_ok, 1)
            for c in range(C):
                to = bank[2 + c // 4][:, :].bitcast(bf16).rearrange("p (c k t) -> p c k t", c=4, k=KB)
                for k in range(KB):
                    ins = pe.transpose(to[:, c % 4, k, :], xq[:, c, k * P:(k + 1) * P], ident_bf[:, :])
                if c % 4 == 3:
                    ins.then_inc(xqT_ps, 1)
            for c in range(C):
                pe.wait_ge(xqT_ok, c // 4 + 1)
                if c >= 4:
                    pe.wait_ge(att_used, c - 3)
                for k in range(KB):
                    ins = pe.matmul(bank[4 + c % 4][:, k * H:(k + 1) * H], xqT[:, c, k, :],
                                    cq[:, (c // CPB) * KB + k, :], start=True, stop=True)
                ins.then_inc(att_ps, 1)
            for c in range(C):
                pe.wait_ge(xf_ok, c + 1)
                for k in range(KB):
                    at = ((c % 2) * KB + k) * P
                    ins = pe.transpose(bank[c // 2][:, at:at + P], xf[:, c, k * P:(k + 1) * P], ident[:, :])
                if c % 2:
                    ins.then_inc(xfT_ps, 1)
            pe.wait_ge(ld_gate, 16)
            for c in range(C):
                pe.wait_ge(xfT_ok, c // 2 + 1)
                for k in range(KB):
                    ins = pe.matmul(bank[4][:, c * E:(c + 1) * E], xfT[:, c, k, :], gate_sb[:, k, :],
                                    start=(k == 0), stop=(k == KB - 1))
            ins.then_inc(logit_ps, 1)

            def shared_gu(u):
                c, h = u // 2, u % 2
                if u >= 2:
                    pe.wait_ge(sh_act, 2 * (u - 1))
                for k in range(KB):
                    ins = pe.matmul(GB[u % 2][:, 0:GU], xfT[:, c, k, :], sgu_sb[:, h, k * GU:(k + 1) * GU],
                                    start=(k == 0), stop=(k == KB - 1))
                ins.then_inc(sh_gu, 1)

            def shared_down(u):
                c, h = u // 2, u % 2
                pe.wait_ge(sh_iTc, u + 1)
                if h == 0 and c >= 2:
                    pe.wait_ge(sh_outc, c - 1)
                pe.matmul(OB[c % 2][:, 0:H], s_iT[0:I0, u % 2, 0, :], sd0_sb[:, h, :], start=(h == 0), stop=False)
                ins = pe.matmul(OB[c % 2][:, 0:H], s_iT[0:I1, u % 2, 1, :], sd1_sb[:, h, :], start=False, stop=(h == 1))
                if h == 1:
                    ins.then_inc(sh_out, 1)

            def shared_unit(u):
                if u + 1 < 2 * C:
                    shared_gu(u + 1)
                if u >= 1:
                    shared_down(u - 1)
                pe.wait_ge(sh_int, u + 1)
                turn(pe, s_int, u % 2, IT[u % 2]).then_inc(sh_iT, 1)

            def counts():
                pe.wait_ge(mask_ok, 1)
                for c in range(C):
                    for d in range(c + 1):
                        pe.matmul(bank[0][:, c * E:(c + 1) * E], (tri_bf if d == c else ones_bf)[:, :], mask_bf[:, d, :],
                                  start=(d == 0), stop=(d == c))
                for c in range(C):
                    ins = pe.matmul(bank[1][0:E, 0:1], mask_bf[:, c, :], ones_bf[:, 0:1], start=(c == 0), stop=(c == C - 1))
                ins.then_inc(cnt_ps, 1)

            def cumulate():
                pe.wait_ge(ntl_ok, 1)
                pe.matmul(bank[1][:, 0:2 * E], ntl_bf[:, :], trie_bf[:, :, :].rearrange("p a e -> p (a e)"), start=True, stop=True)
                pe.matmul(bank[1][0:E, 2 * E:2 * E + 1], trie_bf[:, 0, :], ntl_bf[:, 0:1], start=True, stop=True).then_inc(cum_ps, 1)

            def slot_experts():
                pe.wait_ge(ge_ok, 1)
                pe.matmul(bank[1][0:1, 256:256 + COLS], ones_f[0:E, 0:1], slot_ge[:, :], start=True, stop=True).then_inc(slot_ps, 1)

            def places():
                for n in range(C * 8):
                    c = n // 8
                    if n % 8 == 0:
                        pe.wait_ge(ohj_ok, c + 1)
                        pe.wait_ge(ohp_ok, c + 1)
                    ins = pe.matmul(bank[0][:, 0:COLS], oh_p[:, c, :, n % 8], oh_j[:, c, :, n % 8], start=(n == 0), stop=(n == C * 8 - 1))
                ins.then_inc(tab_ps, 1)

            pe.wait_ge(ld_sh, 48)
            pe.wait_ge(score_ok, 1)
            shared_gu(0)
            between = {4: counts, 5: cumulate, 6: slot_experts, 11: places}
            for u in range(2 * C):
                shared_unit(u)
                if u in between:
                    between[u]()
            shared_down(2 * C - 1)

            def turn_rows(r, b):
                for k in range(KB):
                    ins = pe.transpose(XT[b][:, k * P:(k + 1) * P], rows[:, r, k * P:(k + 1) * P], ident[:, :])
                ins.then_inc(rT_ps, 1)

            def gate_up(r, b):
                for k in range(KB):
                    ins = pe.matmul(GB[b][:, 0:GU], rT[:, b, k, :], gu_ring[:, r, k * GU:(k + 1) * GU],
                                    start=(k == 0), stop=(k == KB - 1))
                ins.then_inc(gu_ps, 1)

            pe.wait_ge(tabs_ok, 1)
            for f in range(2):
                pe.wait_ge(row_in[f], 16)
                turn_rows(f, f)
            pe.wait_ge(gu_in[0], 16)
            pe.wait_ge(rT_ok, 1)
            gate_up(0, 0)
            quads = quads_of(pe)
            with pe.Fori(0, QUADS) as i:
                with pe.If(i < quads):
                    for r in range(R):
                        b = r % 2
                        pe.wait_ge(row_in[(r + 2) % R], i * 16 + (16 if r + 2 < R else 32))
                        turn_rows((r + 2) % R, b)
                        pe.wait_ge(inter_ok, i * R + (r + 1))
                        turn(pe, inter, b, IT[b]).then_inc(iT_ps, 1)
                        pe.wait_ge(gu_in[(r + 1) % R], i * 16 + (16 if r + 1 < R else 32))
                        pe.wait_ge(rT_ok, i * R + (r + 2))
                        gate_up((r + 1) % R, (r + 1) % 2)
                        pe.wait_ge(d_in[r], i * 32 + 32)
                        pe.wait_ge(iT_ok, i * R + (r + 1))
                        pe.matmul(OB[b][:, 0:H], iT[0:I0, b, 0, :], d0_ring[:, r, :], start=True, stop=False)
                        pe.matmul(OB[b][:, 0:H], iT[0:I1, b, 1, :], d1_ring[:, r, :], start=False, stop=True).then_inc(out_ps, 1)



def kernel(x, ctx_2048, L0_ffn_gate_w, L0_ffn_e_bias, L0_ffn_gate_proj, L0_ffn_up_proj, L0_ffn_down_proj,
           L0_ffn_shared_gate_w, L0_ffn_shared_up_w, L0_ffn_shared_down_w):
    import numpy as np
    import concourse.bacc as bacc
    from concourse.bass_utils import run_bass_kernel_spmd

    def arr(a):
        return np.asarray(a)

    def gate_up(gate, up):
        e, i, h = gate.shape
        both = np.concatenate([gate, up], axis=1)
        return both.reshape(e, 2 * i, h // 128, 128).transpose(0, 3, 2, 1).reshape(e, 128, -1)

    xs = arr(x)
    b, s, h = xs.shape
    t = b * s
    gate_w = arr(L0_ffn_gate_w)
    e = gate_w.shape[0]
    down = arr(L0_ffn_down_proj)
    i = down.shape[2]
    host = {
        "x": xs.reshape(t, h),
        "ctx_kn": arr(ctx_2048).transpose(0, 2, 1),
        "gate_kn": gate_w.T,
        "e_bias": arr(L0_ffn_e_bias),
        "w_gu": gate_up(arr(L0_ffn_gate_proj), arr(L0_ffn_up_proj)),
        "w_down": down.transpose(0, 2, 1),
        "ws_gu": gate_up(arr(L0_ffn_shared_gate_w).reshape(2, i, h), arr(L0_ffn_shared_up_w).reshape(2, i, h)),
        "ws_down": arr(L0_ffn_shared_down_w).T.reshape(2, i, h),
    }
    host = {k: np.ascontiguousarray(v) for k, v in host.items()}

    nc = bacc.Bacc("TRN2", target_bir_lowering=False, num_devices=1)
    fp32 = mybir.dt.float32
    ins = [nc.dram_tensor(k, v.shape, mybir.dt.from_np(v.dtype), kind="ExternalInput").ap() for k, v in host.items()]
    xfw = nc.dram_tensor("xfw", (t + 128, h + e), fp32).ap()
    acc = [nc.dram_tensor(f"acc{a}", (t + 128, h), fp32).ap() for a in range(2)]
    out = nc.dram_tensor("out", (t, h), fp32, kind="ExternalOutput").ap()
    xattn_moe_kernel(nc, *ins, xfw, acc, out)
    r = run_bass_kernel_spmd(nc, [host], core_ids=[0])
    return r.results[0]["out"].reshape(b, s, h)
```

```python
import concourse.bass as bass
from concourse import mybir
from contextlib import ExitStack


def xattn_moe_kernel(
    nc: bass.Bass,
    x: bass.AP,
    ctx_kn: bass.AP,
    gate_kn: bass.AP,
    e_bias: bass.AP,
    w_gu: bass.AP,
    w_down: bass.AP,
    ws_gu: bass.AP,
    ws_down: bass.AP,
    xfw: bass.AP,
    acc: list,
    out: bass.AP,
):
    fp32, bf16, fp16, i32 = mybir.dt.float32, mybir.dt.bfloat16, mybir.dt.float16, mybir.dt.int32
    ALU = mybir.AluOpType
    ACT = mybir.ActivationFunctionType
    X = mybir.AxisListType.X

    P = 128
    T, H = x.shape
    BATCH = ctx_kn.shape[0]
    E = gate_kn.shape[1]
    I = w_down.shape[1]
    GU = 2 * I
    C = T // P
    CPB = C // BATCH
    HC = C // 2
    KB = H // P
    TOPK, NGROUP, TOPG = 8, 8, 4
    GSZ = E // NGROUP
    ROW = H + E
    LN_EPS, FP8_MAX, ACT_EPS, W_EPS, SCALE = 1e-5, 448.0, 1e-4, 1e-6, 2.5
    I1 = P // 2
    I0 = I - I1
    IS = ws_down.shape[0]
    SW = [min(P, IS - a) for a in range(0, IS, P)]
    NS = len(SW)
    TH = T // 2
    assert I0 <= P
    MAX_SLOTS = (T * TOPK + E * (P - 1)) // P
    R = 4
    QUADS = -(-MAX_SLOTS // R)
    AHEAD = R + 2
    COLS = R * QUADS + AHEAD
    HALF = 127.0 / 256.0
    ROUND = 1.5 * 2.0 ** 23

    ctx = ExitStack()
    with ctx:
        def sb(name, shape, dt=fp32):
            return ctx.enter_context(nc.sbuf_tensor(name, shape, dt))

        def sem(name):
            return ctx.enter_context(nc.semaphore(name))

        ident = sb("ident", [P, P])
        ident_bf = sb("ident_bf", [P, P], bf16)
        ones_bf = sb("ones_bf", [P, P], bf16)
        tri_bf = sb("tri_bf", [P, P], bf16)
        trie_bf = sb("trie_bf", [E, 2, E], bf16)
        ones_f = sb("ones_f", [P, P])
        tie = sb("tie", [P, NGROUP, NGROUP])
        iota_row = sb("iota_row", [P, COLS])
        part_pad = sb("part_pad", [P, 1])
        token1 = sb("token1", [P, C])
        zeros = sb("zeros", [P, ROW])
        x_sb = sb("x_sb", [P, C, H])
        c_sb = sb("c_sb", [P, BATCH * KB, H])
        gate_sb = sb("gate_sb", [P, KB, E])
        bias_sb = sb("bias_sb", [P, E])
        sgu_sb = sb("sgu_sb", [P, KB, 2 * IS])
        sd_sb = sb("sd_sb", [P, NS, H])
        stats = sb("stats", [P, C, 6])
        mv = sb("mv", [P, C, 2])
        var_e = sb("var_e", [P, C])
        std = sb("std", [P, C])
        rstd = sb("rstd", [P, C])
        nt = sb("nt", [P, C])
        early = sb("early", [P, 3 * C * H])
        ln = early[:, 0:C * H].rearrange("p (c h) -> p c h", c=C)
        qv = early[:, C * H:2 * C * H]
        qm = early[:, 2 * C * H:3 * C * H]
        early_q = sb("early_q", [P, C * H // 2])
        xq = early_q[:, :].bitcast(bf16).rearrange("p (c h) -> p c h", c=C)
        early_cq = sb("early_cq", [P, R * H])
        cq = early_cq[:, 0:BATCH * KB * H // 2].bitcast(bf16).rearrange("p (a n) -> p a n", n=H)
        amax = sb("amax", [P, C * KB])
        qs = sb("qs", [P, C * KB])
        dq = sb("dq", [P, C * KB])
        camax = sb("camax", [P, C * KB])
        cmx = sb("cmx", [16, 1])
        cdiag = sb("cdiag", [16, 16])
        cqs = sb("cqs", [P, C * KB])
        cdq = sb("cdq", [P, C * KB])
        dqq = sb("dqq", [P, C, KB, KB])
        early_c = sb("early_c", [P, 2 * C * H])
        cv = early_c[:, 0:C * H]
        cm = early_c[:, C * H:2 * C * H]
        att = sb("att", [P, 2, H])
        xqT = sb("xqT", [P, C, KB, P], bf16)
        x1 = sb("x1", [P, C, H])
        xf = sb("xf", [P, C, H])
        xfT = sb("xfT", [P, KB, T])
        scores = sb("scores", [P, C, E])
        choice = sb("choice", [P, C, E])
        gtop = sb("gtop", [P, C * NGROUP, 8])
        gsc = sb("gsc", [P, C, NGROUP])
        gcmp = sb("gcmp", [P, C, NGROUP, NGROUP])
        geq = sb("geq", [P, C, NGROUP, NGROUP])
        grank = sb("grank", [P, C * NGROUP])
        gmask = sb("gmask", [P, C * NGROUP])
        masked = sb("masked", [P, C, E])
        top8 = sb("top8", [P, C, 8])
        replaced = sb("replaced", [P, C, E])
        mask = sb("mask", [P, C, E])
        mask_bf = sb("mask_bf", [P, C, E], bf16)
        cw = sb("cw", [P, C, E])
        wsum = sb("wsum", [P, C])
        winv = sb("winv", [P, C])
        cnt = sb("cnt", [E, 1])
        ntl = sb("ntl", [E, 1])
        ntl_bf = sb("ntl_bf", [E, P], bf16)
        base = sb("base", [P, E])
        cum_col = sb("cum_col", [E, 1])
        pos = sb("pos", [P, C, E])
        pos8 = sb("pos8", [P, C, 8])
        posj = sb("posj", [P, C, 8])
        posp = sb("posp", [P, C, 8])
        posj_h = sb("posj_h", [P, C, 8], fp16)
        posp_h = sb("posp_h", [P, C, 8], fp16)
        iota_k = sb("iota_k", [P, COLS, TOPK], fp16)
        oh_p = early_c[:, 0:C * P * TOPK // 2].bitcast(fp16).rearrange("p (c q k) -> p c q k", c=C, k=TOPK)
        oh_s = early[:, 0:C * 8 * COLS // 2].bitcast(fp16).rearrange("p (c j k) -> p c j k", c=C, k=TOPK)
        oh_j = sb("oh_j", [P, C, COLS, TOPK], fp16)
        slot_ge = sb("slot_ge", [E, COLS])
        padv = sb("padv", [P, COLS])
        idx_tab = sb("idx_tab", [P, COLS], i32)
        slot_tab = sb("slot_tab", [1, COLS + 1], i32)
        quads_f = sb("quads_f", [1, 2])
        s_silu = early[:, 3 * C * H - 2 * TH:3 * C * H].rearrange("p (b t) -> p b t", b=2)
        s_up = early_q[:, :].rearrange("p (b t) -> p b t", b=2)
        s_int = sb("s_int", [P, 2 * NS, TH])
        s_out = sb("s_out", [P, 2, H])
        fin = sb("fin", [P, C, H])
        gu_ring = sb("gu_ring", [P, R, KB * GU])
        d0_ring = sb("d0_ring", [I0, R, H])
        d1_ring = sb("d1_ring", [I1, R, H])
        rows = sb("rows", [P, R, ROW])
        wcol = sb("wcol", [P, R])
        gidx = sb("gidx", [P, R], i32)
        sidx = sb("sidx", [P, R], i32)
        rT = sb("rT", [P, 2, KB, P])
        silu = sb("silu", [P, 2, 2 * P])
        inter0 = sb("inter0", [I0, 2, P])
        inter1 = sb("inter1", [I1, 2, P])
        y = early_cq[:, :].rearrange("p (r h) -> p r h", r=R)
        y0, y1 = x_sb, c_sb

        bank = [ctx.enter_context(nc.psum_tensor(f"bank{b}", [P, 512], fp32)) for b in range(8)]
        XT, GB, OB = bank[0:2], bank[2:4], bank[6:8]

        ld_x = [sem(f"ld_x{h}") for h in range(2)]
        ld_c, ld_gate, ld_bias, ld_sh = (sem(n) for n in ("ld_c", "ld_gate", "ld_bias", "ld_sh"))
        cqs_ok, dqq_ok = sem("cqs_ok"), sem("dqq_ok")
        made = sem("made")
        dve = sem("dve")
        ln_var, ln_std = sem("ln_var"), sem("ln_std")
        camax_ok, camaxT_ok, cmx_v, cmx_ok, cbc_ok = (sem(n) for n in ("camax_ok", "camaxT_ok", "cmx_v", "cmx_ok", "cbc_ok"))
        cv_ok, cm_ok, cq_ok, t_ok, tx_ok = (sem(n) for n in ("cv_ok", "cm_ok", "cq_ok", "t_ok", "tx_ok"))
        xq_ok, xqT_ps, xqT_ok, att_ps, att_used = (sem(n) for n in ("xq_ok", "xqT_ps", "xqT_ok", "att_ps", "att_used"))
        xf_ok, xfT_ps, xfT_ok, logit_ps, score_ok = (sem(n) for n in ("xf_ok", "xfT_ps", "xfT_ok", "logit_ps", "score_ok"))
        mask_ok, cnt_ps, ntl_ok, cum_ps = (sem(n) for n in ("mask_ok", "cnt_ps", "ntl_ok", "cum_ps"))
        ohs_ok, ohj_ok, ohp_ok = (sem(n) for n in ("ohs_ok", "ohj_ok", "ohp_ok"))
        tab_ps, ge_ok, slot_ps, tabs_ok = (sem(n) for n in ("tab_ps", "ge_ok", "slot_ps", "tabs_ok"))
        rows_st, cw_ok, zero_ok = sem("rows_st"), sem("cw_ok"), sem("zero_ok")
        sh_gu, sh_act, sh_up, sh_int, sh_out, sh_outc, sh_fin = (
            sem(n) for n in ("sh_gu", "sh_act", "sh_up", "sh_int", "sh_out", "sh_outc", "sh_fin"))
        row_in = [sem(f"row_in{r}") for r in range(R)]
        gu_in = [sem(f"gu_in{r}") for r in range(R)]
        d_in = [sem(f"d_in{r}") for r in range(R)]
        acc_in = [sem(f"acc_in{a}") for a in range(2)]
        pool_go = sem("pool_go")
        wcol_ok = sem("wcol_ok")
        gidx_ok, sidx_ok = sem("gidx_ok"), sem("sidx_ok")
        rT_ps, rT_ok, gu_ps, silu_ok, inter_ok, out_ps, y_ok = (
            sem(n) for n in ("rT_ps", "rT_ok", "gu_ps", "silu_ok", "inter_ok", "out_ps", "y_ok"))
        acc_ld = [sem(f"acc_ld{c}") for c in range(C)]
        y_sum, done = sem("y_sum"), sem("done")

        block = ctx.enter_context(nc.Block())

        def chunks(dram, cols=None):
            return dram[0:T, 0:(cols or dram.shape[1])].rearrange("(c p) h -> p c h", p=P)

        MADE = 17

        def expert_of(eng, slot):
            return eng.value_load(slot_tab[0:1, bass.ds(slot, 1)], min_val=0, max_val=E - 1)

        def load_gu(eng, e, r):
            eng.dma_start(gu_ring[:, r, :], w_gu[bass.ds(e, 1), :, :].rearrange("a p n -> (a p) n")).then_inc(gu_in[r], 16)

        def load_down(eng, e, r):
            eng.dma_start(d0_ring[:, r, :], w_down[bass.ds(e, 1), 0:I0, :].rearrange("a i h -> (a i) h")).then_inc(d_in[r], 16)
            eng.dma_start(d1_ring[:, r, :], w_down[bass.ds(e, 1), I0:I, :].rearrange("a i h -> (a i) h")).then_inc(d_in[r], 16)

        def quads_of(eng):
            return eng.value_load(slot_tab[0:1, COLS:COLS + 1], min_val=1, max_val=QUADS)

        SHARED = ["u0", "u1", "u2", "d0", "u3", "d1", "u4", "d2", "u5", "d3", "d4", "d5", "d6", "d7"]
        ONE_HOTS_AT = {"u5": [0, 1, 2], "d3": [3, 4, 5], "d4": [6, 7]}

        def gather(pool, r):
            pool.wait_ge(rows_st, 48)
            pool.sem_inc(pool_go, 1)
            pool.indirect_dma_start(
                out=rows[:, r, :], out_offset=None, in_=xfw,
                in_offset=bass.IndirectOffsetOnAxis(ap=gidx[:, r:r + 1], axis=0),
                bounds_check=T + P - 1, oob_is_err=True).then_inc(row_in[r], 16)

        def add_chunk(pool, c):
            pool.wait_ge(sh_outc, c + 1)
            pool.tensor_tensor(fin[:, c, :], s_out[:, c % 2, :], x1[:, c, :], ALU.add).then_inc(sh_fin, 1)

        def shared_out(act, c):
            act.wait_ge(sh_out, c + 1)
            if c >= 2:
                act.wait_ge(sh_fin, c - 1)
            act.activation(s_out[:, c % 2, :], OB[c % 2][:, 0:H], ACT.Copy).then_inc(sh_outc, 1)

        def copy_rows(v, e, r, b):
            v.tensor_copy(wcol[:, r:r + 1], rows[:, r, bass.ds(e + H, 1)]).then_inc(wcol_ok, 1)
            v.tensor_copy(rT[:, b, :, :], XT[b][:, 0:H].rearrange("p (k t) -> p k t", k=KB)).then_inc(rT_ok, 1)

        def combine(v, r, count):
            v.wait_ge(silu_ok, count)
            b = r % 2
            v.tensor_tensor(inter0[:, b, :], silu[0:I0, b, 0:P], GB[b][0:I0, 2 * P:3 * P], ALU.mult).then_inc(inter_ok, 1)
            v.tensor_tensor(inter1[:, b, :], silu[0:I1, b, P:2 * P], GB[b][I1:P, P:2 * P], ALU.mult).then_inc(inter_ok, 1)

        def shared_gate(act, u):
            act.wait_ge(sh_gu, u + 1)
            if u >= 2:
                act.wait_ge(sh_int, u - 1)
            w = SW[u % NS]
            act.activation(s_silu[0:w, u % 2, :], bank[2 + 2 * (u % 2)][0:w, :], ACT.Silu).then_inc(sh_act, 1)
            act.activation(s_up[0:w, u % 2, :], bank[3 + 2 * (u % 2)][0:w, :], ACT.Copy).then_inc(sh_up, 1)

        @block.sync
        def _(sp):
            for h in range(2):
                sp.dma_start(x_sb[:, h * HC:(h + 1) * HC, :],
                             x[h * HC * P:(h + 1) * HC * P, :].rearrange("(c p) n -> p c n", p=P)).then_inc(ld_x[h], 16)
            sp.dma_start(gate_sb[:, :, :], gate_kn.rearrange("(k p) e -> p k e", p=P)).then_inc(ld_gate, 16)
            sp.dma_start(bias_sb[:, :], e_bias.partition_broadcast(P)).then_inc(ld_bias, 16)
            sp.dma_start(sgu_sb[:, :, :], ws_gu).then_inc(ld_sh, 16)
            full = IS // P * P
            sp.dma_start(sd_sb[:, 0:IS // P, :], ws_down[0:full, :].rearrange("(s p) h -> p s h", p=P)).then_inc(ld_sh, 16)
            sp.dma_start(sd_sb[0:IS - full, IS // P, :], ws_down[full:IS, :]).then_inc(ld_sh, 16)
            sp.wait_ge(made, MADE)
            sp.dma_start(xfw[T:T + P, :], zeros[:, :]).then_inc(rows_st, 16)
            sp.wait_ge(xf_ok, C)
            sp.dma_start(chunks(xfw, H), xf[:, :, :]).then_inc(rows_st, 16)
            sp.wait_ge(cw_ok, 1)
            sp.dma_start(xfw[0:T, H:ROW].rearrange("(c p) h -> p c h", p=P), cw[:, :, :]).then_inc(rows_st, 16)
            sp.wait_ge(tabs_ok, 1)
            for r in range(R):
                e = expert_of(sp, r)
                load_gu(sp, e, r)
                load_down(sp, e, r)
            quads = quads_of(sp)
            with sp.Fori(0, QUADS) as i:
                with sp.If(i < quads):
                    for r in range(R):
                        e = expert_of(sp, i * R + (r + R))
                        sp.wait_ge(gu_ps, i * R + (r + 1))
                        load_gu(sp, e, r)
                        sp.wait_ge(out_ps, i * R + (r + 1))
                        load_down(sp, e, r)
            for r in range(R):
                sp.wait_ge(gu_in[r], quads * 16 + 16)
                sp.wait_ge(d_in[r], quads * 32 + 32)
            for a in range(2):
                sp.wait_ge(acc_in[a], quads * (16 * R // 2) + 32)
            for c in range(C):
                sp.dma_start(y0[:, c, :], acc[0][c * P:(c + 1) * P, :]).then_inc(acc_ld[c], 16)
                sp.dma_start(y1[:, c, :], acc[1][c * P:(c + 1) * P, :]).then_inc(acc_ld[c], 16)
            for c in range(C):
                sp.wait_ge(y_sum, c + 1)
                sp.dma_start(out[c * P:(c + 1) * P, :], y0[:, c, :]).then_inc(done, 16)
            sp.wait_ge(done, 16 * C)

        @block.gpsimd
        def _(pool):
            steps = [0]

            def step(ins):
                steps[0] += 1
                ins.then_inc(made, 1)

            def cut(t, pattern, mult, op, fill):
                pool.affine_select(out=t, in_=t, compare_op=op, fill=fill, base=0, pattern=pattern,
                                   channel_multiplier=mult).then_inc(made, 1)
                steps[0] += 1

            step(pool.memset(ident[:, :], 0.0))
            step(pool.memset(ident_bf[:, :], 0.0))
            step(pool.memset(tri_bf[:, :], 1.0))
            step(pool.memset(trie_bf[:, :, :], 1.0))
            step(pool.memset(tie[:, :, :], 1.0))
            step(pool.memset(ones_bf[:, :], 1.0))
            step(pool.memset(ones_f[:, :], 1.0))
            step(pool.memset(zeros[:, :], 0.0))
            pool.wait_ge(made, steps[0])
            cut(ident[:, :], [[-1, P]], 1, ALU.not_equal, 1.0)
            cut(ident_bf[:, :], [[-1, P]], 1, ALU.not_equal, 1.0)
            cut(tri_bf[:, :], [[1, P]], -1, ALU.is_gt, 0.0)
            cut(trie_bf[:, :, :], [[-1, 2], [1, E]], -1, ALU.is_ge, 0.0)
            cut(tie[:, :, :], [[1, NGROUP], [-1, NGROUP]], 0, ALU.is_gt, 0.0)
            step(pool.iota(iota_row[:, :], pattern=[[1, COLS]], base=0, channel_multiplier=0,
                           allow_small_or_imprecise_dtypes=True))
            step(pool.iota(iota_k[:, :, :], pattern=[[1, COLS], [0, TOPK]], base=0, channel_multiplier=0,
                           allow_small_or_imprecise_dtypes=True))
            step(pool.iota(part_pad[:, :], pattern=[[0, 1]], base=T + 1, channel_multiplier=1,
                           allow_small_or_imprecise_dtypes=True))
            step(pool.iota(token1[:, :], pattern=[[P, C]], base=1, channel_multiplier=1,
                           allow_small_or_imprecise_dtypes=True))
            assert steps[0] == MADE
            for a in range(2):
                pool.dma_start(acc[a][T:T + P, :], zeros[:, 0:H]).then_inc(acc_in[a], 16)
            pool.dma_start(chunks(acc[1]), zeros[:, 0:H].unsqueeze(1).to_broadcast([P, C, H])).then_inc(acc_in[1], 16)
            pool.wait_ge(cv_ok, C * KB)
            pool.wait_ge(cm_ok, 1)
            pool.tensor_tensor(cv[:, :], cv[:, :], cm[:, :], ALU.add).then_inc(cq_ok, 1)
            pool.wait_ge(cq_ok, 1)
            pool.tensor_tensor(cq[:, :, :].rearrange("p a n -> p (a n)"), cv[:, :], cm[:, :], ALU.subtract).then_inc(cq_ok, 1)
            for c in range(C):
                pool.wait_ge(t_ok, KB * (c + 1))
                pool.tensor_tensor(att[:, c % 2, :], att[:, c % 2, :], x_sb[:, c, :], ALU.add).then_inc(tx_ok, 1)
            for what in SHARED[:-2]:
                n = int(what[1])
                if what[0] == "u":
                    pool.wait_ge(sh_act, n + 1)
                    pool.wait_ge(sh_up, n + 1)
                    w = SW[n % NS]
                    pool.tensor_tensor(s_int[0:w, n, :], s_silu[0:w, n % 2, :], s_up[0:w, n % 2, :], ALU.mult).then_inc(sh_int, 1)
                else:
                    add_chunk(pool, n)
            for r in range(R):
                pool.wait_ge(gidx_ok, r + 1)
                gather(pool, r)
            for c in range(C - 2, C):
                add_chunk(pool, c)
            pool.wait_ge(sh_fin, C)
            pool.dma_start(chunks(acc[0]), fin[:, :, :]).then_inc(acc_in[0], 16)
            for f in range(2):
                pool.wait_ge(gidx_ok, R + f + 1)
                gather(pool, f)
            quads = quads_of(pool)
            with pool.Fori(0, QUADS) as i:
                with pool.If(i < quads):
                    for r in range(R):
                        pool.wait_ge(rT_ok, i * R + (r + 3))
                        pool.wait_ge(gidx_ok, i * R + (r + AHEAD + 1))
                        gather(pool, (r + 2) % R)
                        pool.wait_ge(sidx_ok, i * R + (r + 1))
                        pool.wait_ge(y_ok, i * R + (r + 1))
                        pool.wait_ge(acc_in[r % 2], i * (16 * R // 2) + (32 + 16 * (r // 2)))
                        pool.sem_inc(pool_go, 1)
                        pool.indirect_dma_start(
                            out=acc[r % 2], out_offset=bass.IndirectOffsetOnAxis(ap=sidx[:, r:r + 1], axis=0),
                            in_=y[:, r, :], in_offset=None, bounds_check=T + P - 1, oob_is_err=True,
                            compute_op=ALU.add).then_inc(acc_in[r % 2], 16)
            for r in range(R):
                pool.wait_ge(row_in[r], quads * 16 + (32 if r < 2 else 16))

        @block.scalar
        def _(act):
            act.dma_start(c_sb[:, :, :], ctx_kn.rearrange("b (k p) n -> p (b k) n", p=P)).then_inc(ld_c, 16)
            act.wait_ge(ln_var, 1)
            act.activation(std[:, :], var_e[:, :], ACT.Sqrt).then_inc(ln_std, 1)
            act.wait_ge(cqs_ok, 1)
            act.wait_ge(ld_c, 16)
            for s in range(C * KB):
                a, n = s // KB, s % KB
                act.activation(cv[:, s * P:(s + 1) * P], c_sb[:, a, n * P:(n + 1) * P], ACT.Copy,
                               scale=cqs[:, s:s + 1]).then_inc(cv_ok, 1)

            def second_root(h):
                act.wait_ge(ln_var, 2 + h)
                act.activation(std[:, h * HC:(h + 1) * HC], var_e[:, h * HC:(h + 1) * HC], ACT.Sqrt).then_inc(ln_std, 1)

            act.wait_ge(dqq_ok, CPB)
            for h in range(2):
                act.wait_ge(xqT_ps, h + 1)
                act.activation(xqT[:, h * HC:(h + 1) * HC, :, :], bank[2 + h][:, :].bitcast(bf16).rearrange(
                    "p (c k t) -> p c k t", c=HC, k=KB), ACT.Copy).then_inc(xqT_ok, 1)
                for c in range(h * HC, (h + 1) * HC):
                    act.wait_ge(att_ps, 2 * c + 1)
                    if c >= 2:
                        act.wait_ge(att_used, c - 1)
                    for n in range(KB):
                        act.activation(att[:, c % 2, n * P:(n + 1) * P], bank[4 + c % 2][:, n * P:(n + 1) * P], ACT.Copy,
                                       scale=dqq[:, c, 0, n:n + 1]).then_inc(t_ok, 1)
                    if c == HC + 1:
                        second_root(0)
            second_root(1)
            for h in range(2):
                for b in range(h * HC // 2, (h + 1) * HC // 2):
                    act.wait_ge(xfT_ps, b + 1)
                    act.activation(xfT[:, :, 2 * b * P:(2 * b + 2) * P].rearrange("p k (c t) -> p c k t", t=P),
                                   bank[b][:, :].rearrange("p (c k t) -> p c k t", c=2, k=KB), ACT.Copy).then_inc(xfT_ok, 1)
                act.wait_ge(logit_ps, h + 1)
                act.activation(scores[:, h * HC:(h + 1) * HC, :], bank[4 + h][:, 0:HC * E].rearrange(
                    "p (c e) -> p c e", c=HC), ACT.Sigmoid).then_inc(score_ok, 1)
            for what in SHARED:
                if what[0] == "u":
                    shared_gate(act, int(what[1]))
                else:
                    shared_out(act, int(what[1]))
                for c in ONE_HOTS_AT.get(what, []):
                    act.wait_ge(ohs_ok, c + 1)
                    act.activation(oh_j[:, c, :, :], oh_s[:, c, :, :], ACT.Copy,
                                   scale=token1[:, c:c + 1]).then_inc(ohj_ok, 1)
            act.wait_ge(gu_ps, 1)
            act.activation(silu[:, 0, :], GB[0][:, 0:2 * P], ACT.Silu).then_inc(silu_ok, 1)
            act.wait_ge(tabs_ok, 1)
            quads = quads_of(act)
            with act.Fori(0, QUADS) as i:
                with act.If(i < quads):
                    for r in range(R):
                        act.wait_ge(gu_ps, i * R + (r + 2))
                        act.activation(silu[:, (r + 1) % 2, :], GB[(r + 1) % 2][:, 0:2 * P], ACT.Silu).then_inc(silu_ok, 1)
                        act.wait_ge(acc_in[r % 2], i * (16 * R // 2) + 16 * (r // 2 + 1))
                        act.wait_ge(wcol_ok, i * R + (r + 1))
                        act.wait_ge(out_ps, i * R + (r + 1))
                        act.activation(y[:, r, :], OB[r % 2][:, 0:H], ACT.Copy, scale=wcol[:, r:r + 1]).then_inc(y_ok, 1)

        @block.vector
        def _(v):
            made_by = [0]

            def step(ins):
                made_by[0] += 1
                ins.then_inc(dve, 1)

            def settle():
                v.wait_ge(dve, made_by[0])

            def norm_stats(src, c0, c1):
                for c in range(c0, c1):
                    step(v.bn_stats(stats[:, c, :], src[:, c, :]))
                settle()
                for c in range(c0, c1):
                    step(v.bn_aggr(mv[:, c, :], stats[:, c, :]))
                settle()
                v.tensor_scalar(var_e[:, c0:c1], mv[:, c0:c1, 1], LN_EPS, None, ALU.add).then_inc(ln_var, 1)

            def norm_rstd(c0, c1, n):
                cs = slice(c0, c1)
                v.wait_ge(ln_var, n)
                v.wait_ge(ln_std, n)
                step(v.reciprocal(rstd[:, cs], std[:, cs]))
                settle()
                step(v.tensor_tensor(nt[:, cs], rstd[:, cs], rstd[:, cs], ALU.mult))
                settle()
                step(v.scalar_tensor_tensor(nt[:, cs], nt[:, cs], -0.5, var_e[:, cs], ALU.mult, ALU.mult))
                settle()
                step(v.scalar_tensor_tensor(rstd[:, cs], nt[:, cs], 1.5, rstd[:, cs], ALU.add, ALU.mult))
                settle()

            def normalise(dst, src, c):
                return v.tensor_scalar(dst[:, c, :], src[:, c, :], mv[:, c, 0:1], rstd[:, c:c + 1],
                                       ALU.subtract, ALU.mult)

            def magnitude(to, of):
                step(v.tensor_scalar(to.bitcast(i32), of.bitcast(i32), 0x7F800000, None, ALU.bitwise_and))
                settle()
                return v.tensor_scalar(to, to, 2.0 ** -6, 1.5 * 2.0 ** 20, ALU.max, ALU.mult)

            def scales(src, floor, mul, div, to):
                step(v.tensor_scalar(div[:, :], src, floor, None, ALU.max))
                settle()
                step(v.reciprocal(mul[:, :], div[:, :]))
                settle()
                v.tensor_scalar(mul[:, :], mul[:, :], FP8_MAX, None, ALU.mult).then_inc(to, 1)
                v.tensor_scalar(div[:, :], div[:, :], 1.0 / FP8_MAX, None, ALU.mult).then_inc(to, 1)

            for h in range(2):
                v.wait_ge(ld_x[h], 16)
                for c in range(h * HC, (h + 1) * HC):
                    step(v.bn_stats(stats[:, c, :], x_sb[:, c, :]))
            settle()
            for c in range(C):
                step(v.bn_aggr(mv[:, c, :], stats[:, c, :]))
            settle()
            v.tensor_scalar(var_e[:, :], mv[:, :, 1], LN_EPS, None, ALU.add).then_inc(ln_var, 1)
            v.wait_ge(ld_c, 16)
            v.tensor_reduce(camax[:, :], c_sb[:, :, :].rearrange("p a (n m) -> p (a n) m", m=P), X, ALU.max,
                            apply_absolute_value=True).then_inc(camax_ok, 1)
            norm_rstd(0, C, 1)
            for c in range(HC):
                step(normalise(ln, x_sb, c))
            v.wait_ge(camaxT_ok, 1)
            v.tensor_reduce(cmx[:, :], bank[0][0:16, 0:P], X, ALU.max).then_inc(cmx_v, 1)
            v.wait_ge(cmx_v, 1)
            v.tensor_scalar(cdiag[:, :], ident[0:16, 0:16], cmx[:, 0:1], None, ALU.mult).then_inc(cmx_ok, 1)
            for c in range(HC, C):
                step(normalise(ln, x_sb, c))
            v.wait_ge(cbc_ok, 1)
            scales(bank[1][:, 0:C * KB], W_EPS, cqs, cdq, cqs_ok)
            ln_seg = ln.rearrange("p c (k m) -> p (c k) m", m=P)
            step(v.tensor_reduce(amax[:, :], ln_seg, X, ALU.max, apply_absolute_value=True))
            settle()
            scales(amax[:, :], ACT_EPS, qs, dq, dve)
            made_by[0] += 2
            settle()
            for h in range(2):
                ss, es = slice(h * C, (h + 1) * C), slice(h * HC * H, (h + 1) * HC * H)
                step(v.tensor_tensor(qv[:, es].rearrange("p (s n) -> p s n", n=P), ln_seg[:, ss, :],
                                     qs[:, ss].unsqueeze(2).to_broadcast([P, C, P]), ALU.mult))
                settle()
                step(magnitude(qm[:, es], qv[:, es]))
                settle()
                step(v.tensor_tensor(qv[:, es], qv[:, es], qm[:, es], ALU.add))
                settle()
                v.tensor_tensor(xq[:, h * HC:(h + 1) * HC, :].rearrange("p c n -> p (c n)"), qv[:, es], qm[:, es],
                                ALU.subtract).then_inc(xq_ok, 1)
                if h == 0:
                    v.wait_ge(cv_ok, C * KB)
                    magnitude(cm[:, :], cv[:, :]).then_inc(cm_ok, 1)
            v.wait_ge(cqs_ok, 2)
            for h in range(CPB):
                v.tensor_tensor(
                    dqq[:, h::CPB, :, :], dq[:, :].rearrange("p (c k) -> p c k", k=KB)[:, h::CPB, :].unsqueeze(3)
                    .to_broadcast([P, BATCH, KB, KB]), cdq[:, :].rearrange("p (b k n) -> p b k n", b=BATCH, k=KB),
                    ALU.mult).then_inc(dqq_ok, 1)
            v.wait_ge(dqq_ok, CPB)

            def attend(c):
                v.wait_ge(att_ps, 2 * c + 2)
                v.wait_ge(tx_ok, c + 1)
                for n in range(KB):
                    cols = slice(n * P, (n + 1) * P)
                    ins = v.scalar_tensor_tensor(x1[:, c, cols], bank[6 + c % 2][:, cols], dqq[:, c, 1, n:n + 1],
                                                 att[:, c % 2, cols], ALU.mult, ALU.add)
                    if n == KB - 1:
                        ins.then_inc(att_used, 1)
                    else:
                        step(ins)

            for c in range(HC):
                attend(c)
            v.wait_ge(att_used, HC)
            settle()
            norm_stats(x1, 0, HC)
            attend(HC)
            norm_rstd(0, HC, 2)
            for c in range(HC):
                normalise(xf, x1, c).then_inc(xf_ok, 1)
            for c in range(HC + 1, C):
                attend(c)
            v.wait_ge(att_used, C)
            settle()
            norm_stats(x1, HC, C)
            norm_rstd(HC, C, 3)
            for c in range(HC, C):
                normalise(xf, x1, c).then_inc(xf_ok, 1)

            v.wait_ge(ld_bias, 16)
            for h in range(2):
                cs, gs = slice(h * HC, (h + 1) * HC), slice(h * HC * NGROUP, (h + 1) * HC * NGROUP)
                v.wait_ge(score_ok, h + 1)
                step(v.tensor_tensor(choice[:, cs, :], scores[:, cs, :], bias_sb[:, :].unsqueeze(1).to_broadcast([P, HC, E]), ALU.add))
                settle()
                for c in range(h * HC, (h + 1) * HC):
                    for g in range(NGROUP):
                        step(v.max(gtop[:, c * NGROUP + g, :], choice[:, c, g * GSZ:(g + 1) * GSZ]))
                settle()
                step(v.tensor_tensor(gsc[:, cs, :].rearrange("p c g -> p (c g)"), gtop[:, gs, 0], gtop[:, gs, 1], ALU.add))
                settle()
                shape = [P, HC, NGROUP, NGROUP]
                other, own = gsc[:, cs, :].unsqueeze(2).to_broadcast(shape), gsc[:, cs, :].unsqueeze(3).to_broadcast(shape)
                step(v.tensor_tensor(gcmp[:, cs, :, :], other, own, ALU.is_gt))
                step(v.tensor_tensor(geq[:, cs, :, :], other, own, ALU.is_equal))
                settle()
                step(v.tensor_tensor(geq[:, cs, :, :], geq[:, cs, :, :], tie[:, :, :].unsqueeze(1).to_broadcast(shape), ALU.mult))
                settle()
                step(v.tensor_tensor(gcmp[:, cs, :, :], gcmp[:, cs, :, :], geq[:, cs, :, :], ALU.add))
                settle()
                step(v.tensor_reduce(grank[:, gs], gcmp[:, cs, :, :].rearrange("p c g o -> p (c g) o"), X, ALU.add))
                settle()
                step(v.tensor_scalar(gmask[:, gs], grank[:, gs], float(TOPG), None, ALU.is_lt))
                settle()
                step(v.tensor_tensor(masked[:, cs, :].rearrange("p c (g s) -> p (c g) s", s=GSZ),
                                     choice[:, cs, :].rearrange("p c (g s) -> p (c g) s", s=GSZ),
                                     gmask[:, gs].unsqueeze(2).to_broadcast([P, HC * NGROUP, GSZ]), ALU.mult))
                settle()
                for c in range(h * HC, (h + 1) * HC):
                    step(v.max(top8[:, c, :], masked[:, c, :]))
                settle()
                for c in range(h * HC, (h + 1) * HC):
                    step(v.match_replace(replaced[:, c, :], top8[:, c, :], masked[:, c, :], -3.0e38))
                settle()
                v.tensor_tensor(mask_bf[:, cs, :], replaced[:, cs, :], masked[:, cs, :], ALU.not_equal).then_inc(mask_ok, 1)
                step(v.tensor_tensor(mask[:, cs, :], replaced[:, cs, :], masked[:, cs, :], ALU.not_equal))
                settle()
            v.wait_ge(cnt_ps, 1)
            step(v.tensor_scalar(cnt[:, :], bank[1][0:E, 0:1], 1.0 / P, (P - 1.0) / P - HALF, ALU.mult, ALU.add))
            settle()
            step(v.tensor_scalar(ntl[:, :], cnt[:, :], ROUND, ROUND, ALU.add, ALU.subtract))
            settle()
            v.tensor_copy(ntl_bf[:, :], ntl[:, 0:1].to_broadcast([E, P])).then_inc(ntl_ok, 1)
            v.wait_ge(cum_ps, 1)
            step(v.tensor_scalar(base[:, :], bank[1][:, E:2 * E], float(P), 1.0, ALU.mult, ALU.add))
            step(v.tensor_copy(cum_col[:, :], bank[1][0:E, 2 * E:2 * E + 1]))
            step(v.tensor_scalar(quads_f[:, 0:1], bank[1][0:1, E - 1:E], 1.0 / R, (R - 1.0) / R - 0.375, ALU.mult, ALU.add))
            settle()
            step(v.tensor_tensor(pos[:, :, :], bank[0][:, :].rearrange("p (c e) -> p c e", c=C),
                                 base[:, :].unsqueeze(1).to_broadcast([P, C, E]), ALU.add))
            v.tensor_scalar(slot_ge[:, :], iota_row[0:E, :], cum_col[:, 0:1], None, ALU.is_ge).then_inc(ge_ok, 1)
            settle()
            step(v.tensor_tensor(pos[:, :, :], pos[:, :, :], mask[:, :, :], ALU.mult))
            settle()
            for c in range(C):
                step(v.max(pos8[:, c, :], pos[:, c, :]))
            settle()
            step(v.tensor_scalar(posj[:, :, :], pos8[:, :, :], 1.0 / P, -1.0 / P - HALF, ALU.mult, ALU.add))
            settle()
            step(v.tensor_scalar(posj[:, :, :], posj[:, :, :], ROUND, ROUND, ALU.add, ALU.subtract))
            settle()
            step(v.tensor_copy(posj_h[:, :, :], posj[:, :, :]))
            step(v.tensor_scalar(posp[:, :, :], posj[:, :, :], -float(P), -1.0, ALU.mult, ALU.add))
            settle()
            step(v.tensor_tensor(posp_h[:, :, :], posp[:, :, :], pos8[:, :, :], ALU.add))
            settle()
            for c in range(C):
                v.tensor_tensor(oh_s[:, c, :, :], posj_h[:, c, :].unsqueeze(1).to_broadcast([P, COLS, TOPK]),
                                iota_k[:, :, :], ALU.is_equal).then_inc(ohs_ok, 1)
                v.tensor_tensor(oh_p[:, c, :, :], posp_h[:, c, :].unsqueeze(1).to_broadcast([P, P, TOPK]),
                                iota_k[:, 0:P, :], ALU.is_equal).then_inc(ohp_ok, 1)
            step(v.tensor_tensor(cw[:, :, :], scores[:, :, :], mask[:, :, :], ALU.mult))
            settle()
            step(v.tensor_reduce(wsum[:, :], cw[:, :, :], X, ALU.add))
            settle()
            step(v.tensor_scalar(wsum[:, :], wsum[:, :], 1e-20, None, ALU.add))
            settle()
            step(v.reciprocal(winv[:, :], wsum[:, :]))
            settle()
            step(v.tensor_scalar(winv[:, :], winv[:, :], SCALE, None, ALU.mult))
            settle()
            v.tensor_tensor(cw[:, :, :], cw[:, :, :], winv[:, :].unsqueeze(2).to_broadcast([P, C, E]), ALU.mult).then_inc(cw_ok, 1)
            v.wait_ge(slot_ps, 1)
            step(v.tensor_scalar(slot_tab[:, 0:COLS], bank[1][0:1, 256:256 + COLS], E - 1.0, None, ALU.min))
            step(v.tensor_scalar(slot_tab[:, COLS:COLS + 1], quads_f[:, 0:1], ROUND, ROUND, ALU.add, ALU.subtract))
            v.wait_ge(tab_ps, 1)
            step(v.tensor_scalar(padv[:, :], bank[0][:, 0:COLS], 0.0, part_pad[:, 0:1], ALU.is_equal, ALU.mult))
            settle()
            v.scalar_tensor_tensor(idx_tab[:, :], bank[0][:, 0:COLS], -1.0, padv[:, :], ALU.add, ALU.add).then_inc(tabs_ok, 1)

            v.wait_ge(tabs_ok, 1)
            for r in range(R):
                v.tensor_copy(gidx[:, r:r + 1], idx_tab[:, r:r + 1]).then_inc(gidx_ok, 1)
            quads = quads_of(v)
            for f in range(2):
                v.wait_ge(rT_ps, f + 1)
                copy_rows(v, expert_of(v, f), f, f)
                v.tensor_copy(gidx[:, f:f + 1], idx_tab[:, R + f:R + f + 1]).then_inc(gidx_ok, 1)
            combine(v, 0, 1)
            with v.Fori(0, QUADS) as i:
                with v.If(i < quads):
                    for r in range(R):
                        e = expert_of(v, i * R + (r + 2))
                        v.wait_ge(acc_in[r % 2], i * (16 * R // 2) + 16 * (r // 2 + 1))
                        v.tensor_copy(sidx[:, r:r + 1], idx_tab[:, bass.ds(i * R + r, 1)]).then_inc(sidx_ok, 1)
                        v.wait_ge(rT_ps, i * R + (r + 3))
                        g = (r + 2) % R
                        v.tensor_copy(gidx[:, g:g + 1], idx_tab[:, bass.ds(i * R + (r + AHEAD), 1)]).then_inc(gidx_ok, 1)
                        copy_rows(v, e, g, r % 2)
                        combine(v, (r + 1) % R, i * R + (r + 2))
            for c in range(C):
                v.wait_ge(acc_ld[c], 32)
                v.tensor_tensor(y0[:, c, :], y0[:, c, :], y1[:, c, :], ALU.add).then_inc(y_sum, 1)

        @block.tensor
        def _(pe):
            pe.wait_ge(made, MADE)
            pe.wait_ge(camax_ok, 1)
            pe.transpose(bank[0][0:16, 0:P], camax[:, :], ident[:, :]).then_inc(camaxT_ok, 1)
            pe.wait_ge(cmx_ok, 1)
            pe.matmul(bank[1][:, 0:16], ones_f[0:16, :], cdiag[:, :], start=True, stop=True).then_inc(cbc_ok, 1)
            pe.wait_ge(cq_ok, 2)
            for h in range(2):
                pe.wait_ge(xq_ok, h + 1)
                to = bank[2 + h][:, :].bitcast(bf16).rearrange("p (c k t) -> p c k t", c=HC, k=KB)
                for c in range(HC):
                    for k in range(KB):
                        ins = pe.transpose(to[:, c, k, :], xq[:, h * HC + c, k * P:(k + 1) * P], ident_bf[:, :])
                ins.then_inc(xqT_ps, 1)
            for c in range(C):
                pe.wait_ge(xqT_ok, c // HC + 1)
                if c >= 2:
                    pe.wait_ge(att_used, c - 1)
                for k in range(KB):
                    pe.matmul(bank[4 + 2 * k + c % 2][:, 0:H], xqT[:, c, k, :],
                              cq[:, (c // CPB) * KB + k, :], start=True, stop=True).then_inc(att_ps, 1)

            def turn_normalised(h):
                for c in range(h * HC, (h + 1) * HC):
                    pe.wait_ge(xf_ok, c + 1)
                    for k in range(KB):
                        at = ((c % 2) * KB + k) * P
                        ins = pe.transpose(bank[c // 2][:, at:at + P], xf[:, c, k * P:(k + 1) * P], ident[:, :])
                    if c % 2:
                        ins.then_inc(xfT_ps, 1)

            def logits(h):
                pe.wait_ge(ld_gate, 16)
                for c in range(h * HC, (h + 1) * HC):
                    pe.wait_ge(xfT_ok, c // 2 + 1)
                    at = (c - h * HC) * E
                    for k in range(KB):
                        ins = pe.matmul(bank[4 + h][:, at:at + E], xfT[:, k, c * P:(c + 1) * P], gate_sb[:, k, :],
                                        start=(k == 0), stop=(k == KB - 1))
                ins.then_inc(logit_ps, 1)

            for h in range(2):
                turn_normalised(h)
                logits(h)

            def shared_gate_up(u):
                h, s = u // NS, u % NS
                if u >= 2:
                    pe.wait_ge(sh_up, u - 1)
                    pe.wait_ge(sh_act, u - 1)
                elif u == 1:
                    pe.wait_ge(score_ok, 2)
                for which in range(2):
                    for k in range(KB):
                        at = which * IS + s * P
                        ins = pe.matmul(bank[2 + which + 2 * (u % 2)][0:SW[s], :], sgu_sb[:, k, at:at + SW[s]],
                                        xfT[:, k, h * TH:(h + 1) * TH], start=(k == 0), stop=(k == KB - 1))
                ins.then_inc(sh_gu, 1)

            def shared_down(c):
                h, at = c // HC, (c % HC) * P
                pe.wait_ge(sh_int, NS * (h + 1))
                if c >= 2:
                    pe.wait_ge(sh_outc, c - 1)
                for s in range(NS):
                    ins = pe.matmul(OB[c % 2][:, 0:H], s_int[0:SW[s], h * NS + s, at:at + P], sd_sb[0:SW[s], s, :],
                                    start=(s == 0), stop=(s == NS - 1))
                ins.then_inc(sh_out, 1)

            def counts():
                pe.wait_ge(mask_ok, 2)
                for c in range(C):
                    for d in range(c + 1):
                        pe.matmul(bank[0][:, c * E:(c + 1) * E], (tri_bf if d == c else ones_bf)[:, :], mask_bf[:, d, :],
                                  start=(d == 0), stop=(d == c))
                for c in range(C):
                    ins = pe.matmul(bank[1][0:E, 0:1], mask_bf[:, c, :], ones_bf[:, 0:1], start=(c == 0), stop=(c == C - 1))
                ins.then_inc(cnt_ps, 1)

            def cumulate():
                pe.wait_ge(ntl_ok, 1)
                pe.matmul(bank[1][:, 0:2 * E], ntl_bf[:, :], trie_bf[:, :, :].rearrange("p a e -> p (a e)"), start=True, stop=True)
                pe.matmul(bank[1][0:E, 2 * E:2 * E + 1], trie_bf[:, 0, :], ntl_bf[:, 0:1], start=True, stop=True).then_inc(cum_ps, 1)

            def slot_experts():
                pe.wait_ge(ge_ok, 1)
                pe.matmul(bank[1][0:1, 256:256 + COLS], ones_f[0:E, 0:1], slot_ge[:, :], start=True, stop=True).then_inc(slot_ps, 1)

            def places():
                for n in range(C * 8):
                    c = n // 8
                    if n % 8 == 0:
                        pe.wait_ge(ohj_ok, c + 1)
                        pe.wait_ge(ohp_ok, c + 1)
                    ins = pe.matmul(bank[0][:, 0:COLS], oh_p[:, c, :, n % 8], oh_j[:, c, :, n % 8], start=(n == 0), stop=(n == C * 8 - 1))
                ins.then_inc(tab_ps, 1)

            pe.wait_ge(ld_sh, 48)
            between = {"u2": [counts], "d0": [cumulate], "u3": [slot_experts], "d5": [places]}
            for what in SHARED:
                (shared_gate_up if what[0] == "u" else shared_down)(int(what[1]))
                for routing in between.get(what, []):
                    routing()

            def turn_rows(r, b):
                for k in range(KB):
                    ins = pe.transpose(XT[b][:, k * P:(k + 1) * P], rows[:, r, k * P:(k + 1) * P], ident[:, :])
                ins.then_inc(rT_ps, 1)

            def gate_up(r, b):
                for n, (at, m) in enumerate(((0, P), (I0, P), (I0 + P, I0))):
                    for k in range(KB):
                        ins = pe.matmul(GB[b][0:m, n * P:(n + 1) * P], gu_ring[:, r, k * GU + at:k * GU + at + m], rT[:, b, k, :],
                                        start=(k == 0), stop=(k == KB - 1))
                ins.then_inc(gu_ps, 1)

            pe.wait_ge(tabs_ok, 1)
            for f in range(2):
                pe.wait_ge(row_in[f], 16)
                turn_rows(f, f)
            pe.wait_ge(gu_in[0], 16)
            pe.wait_ge(rT_ok, 1)
            gate_up(0, 0)
            quads = quads_of(pe)
            with pe.Fori(0, QUADS) as i:
                with pe.If(i < quads):
                    for r in range(R):
                        b = r % 2
                        pe.wait_ge(row_in[(r + 2) % R], i * 16 + (16 if r + 2 < R else 32))
                        turn_rows((r + 2) % R, b)
                        pe.wait_ge(gu_in[(r + 1) % R], i * 16 + (16 if r + 1 < R else 32))
                        pe.wait_ge(rT_ok, i * R + (r + 2))
                        gate_up((r + 1) % R, (r + 1) % 2)
                        pe.wait_ge(d_in[r], i * 32 + 32)
                        pe.wait_ge(inter_ok, i * (2 * R) + (2 * r + 2))
                        pe.matmul(OB[b][:, 0:H], inter0[:, b, :], d0_ring[:, r, :], start=True, stop=False)
                        pe.matmul(OB[b][:, 0:H], inter1[:, b, :], d1_ring[:, r, :], start=False, stop=True).then_inc(out_ps, 1)



def kernel(x, ctx_2048, L0_ffn_gate_w, L0_ffn_e_bias, L0_ffn_gate_proj, L0_ffn_up_proj, L0_ffn_down_proj,
           L0_ffn_shared_gate_w, L0_ffn_shared_up_w, L0_ffn_shared_down_w):
    import numpy as np
    import concourse.bacc as bacc
    from concourse.bass_utils import run_bass_kernel_spmd

    def arr(a):
        return np.asarray(a)

    def by_half(w):
        return w.reshape(w.shape[0], w.shape[1] // 128, 128).transpose(2, 1, 0)

    def gate_up(gate, up):
        return by_half(np.concatenate([gate, up[-64:], up[:-64]])).reshape(128, -1)

    xs = arr(x)
    b, s, h = xs.shape
    t = b * s
    gate_w = arr(L0_ffn_gate_w)
    e = gate_w.shape[0]
    down = arr(L0_ffn_down_proj)
    i = down.shape[2]
    host = {
        "x": xs.reshape(t, h),
        "ctx_kn": arr(ctx_2048).transpose(0, 2, 1),
        "gate_kn": gate_w.T,
        "e_bias": arr(L0_ffn_e_bias),
        "w_gu": np.stack([gate_up(g, u) for g, u in zip(arr(L0_ffn_gate_proj), arr(L0_ffn_up_proj))]),
        "w_down": down.transpose(0, 2, 1),
        "ws_gu": by_half(np.concatenate([arr(L0_ffn_shared_gate_w), arr(L0_ffn_shared_up_w)])),
        "ws_down": arr(L0_ffn_shared_down_w).T,
    }
    host = {k: np.ascontiguousarray(v) for k, v in host.items()}

    nc = bacc.Bacc("TRN2", target_bir_lowering=False, num_devices=1)
    fp32 = mybir.dt.float32
    ins = [nc.dram_tensor(k, v.shape, mybir.dt.from_np(v.dtype), kind="ExternalInput").ap() for k, v in host.items()]
    xfw = nc.dram_tensor("xfw", (t + 128, h + e), fp32).ap()
    acc = [nc.dram_tensor(f"acc{a}", (t + 128, h), fp32).ap() for a in range(2)]
    out = nc.dram_tensor("out", (t, h), fp32, kind="ExternalOutput").ap()
    xattn_moe_kernel(nc, *ins, xfw, acc, out)
    r = run_bass_kernel_spmd(nc, [host], core_ids=[0])
    return r.results[0]["out"].reshape(b, s, h)
```
